# Optimizing a Trainium2 kernel written in Bass

```python
import numpy as np
import jax
import jax.numpy as jnp

def _softmax(x, axis=-1):
    return jax.nn.softmax(x, axis=axis)

def _gelu(x):
    return jax.nn.gelu(x, approximate=True)

def _silu(x):
    return jax.nn.silu(x)

def _sigmoid(x):
    return jax.nn.sigmoid(x)

def _layernorm(x, axis=-1, eps=1e-05):
    m = jnp.mean(x, axis=axis, keepdims=True)
    v = jnp.var(x, axis=axis, keepdims=True)
    return (x - m) / jnp.sqrt(v + eps)

def _scatter_add(tgt, idx, src, axis=0):
    return tgt.at[idx].add(src)

def _segment_sum(src, seg, n):
    return jax.ops.segment_sum(src, seg, n)
kernel_name = 'mk_xattn_ffn_d2_seqx_r4_cd9521'

def setup_inputs(seed: int=0):
    np.random.seed(seed)
    _w = jnp.asarray

    def _rec_inputs():
        import jax
        import jax.numpy as jnp
        _rk = jax.random.key(seed)
        x = -0.000125 + 0.9999 * jax.random.normal(jax.random.fold_in(_rk, 1), (8, 512, 256), jnp.float32)
        _lenS = 512 - jax.random.randint(jax.random.fold_in(_rk, 7), (8,), 0, max(1, 512 // 4) + 1, jnp.int32)
        _lenS2 = 512 - jax.random.randint(jax.random.fold_in(_rk, 8), (8,), 0, max(1, 512 // 4) + 1, jnp.int32)
        _ctx_1024P = jax.random.normal(jax.random.fold_in(_rk, 11), (8, 16, 256), jnp.float32)
        _ctx_1024c = jax.random.dirichlet(jax.random.fold_in(_rk, 511), 0.3 * jnp.ones((16,), jnp.float32), (8, 512))
        _ctx_1024t = jnp.einsum('bsk,bkd->bsd', _ctx_1024c, _ctx_1024P)
        _ctx_1024t = _ctx_1024t * jax.lax.rsqrt(jnp.mean(jnp.square(_ctx_1024t)) + 1e-12) * 0.953939
        ctx_1024 = -1.52775e-05 + 0.999936 * (_ctx_1024t + 0.3 * jax.random.normal(jax.random.fold_in(_rk, 611), (8, 512, 256), jnp.float32))
        _validS = jnp.arange(512)[None, :] < _lenS[:, None]
        _validS2 = jnp.arange(512)[None, :] < _lenS2[:, None]
        _causal = jnp.tril(jnp.ones((512, 512), dtype=bool))
        mask_BxSxS2_if1 = jnp.where(jnp.ones((8, 512, 512), dtype=bool), 1, 0).astype(jnp.int32)
        return (x, ctx_1024, mask_BxSxS2_if1)
    x, ctx_1024, mask_BxSxS2_if1 = _rec_inputs()

    def _L0_xattn_setup():
        import jax, jax.numpy as jnp
        import numpy as np
        EMBED_SIZE = 256
        B, S, E = (8, 1024, EMBED_SIZE)

        def _feature_map(x):
            return jax.nn.gelu(x, approximate=False) + 1.0
        key = jax.random.key(seed)
        k1, k2, k3 = jax.random.split(key, 3)
        query = jax.random.normal(k1, (B, S, E), dtype=jnp.float32)
        keys = jax.random.normal(k2, (B, S, E), dtype=jnp.float32)
        values = jax.random.normal(k3, (B, S, E), dtype=jnp.float32)
        return {'query': query, 'keys': keys, 'values': values}
    _L0_xattn_all = _L0_xattn_setup()
    _L0_xattn_in = {k: v for k, v in _L0_xattn_all.items() if k in ()}
    del _L0_xattn_all

    def _L0_ffn_setup():
        import jax, jax.numpy as jnp
        import numpy as np
        TOP_K = 2
        key = jax.random.key(seed)
        k1, k2, k3, k4 = jax.random.split(key, 4)
        B, S, H, I, E = (2, 512, 256, 1024, 8)
        return {'hidden_states': jax.random.normal(k1, (B, S, H), jnp.float32), 'gate_w': jax.random.normal(k2, (E, H), jnp.float32) * 0.02, 'gate_up_proj': jax.random.normal(k3, (E, 2 * I, H), jnp.float32) * 0.02, 'down_proj': jax.random.normal(k4, (E, H, I), jnp.float32) * 0.02}
    _L0_ffn_all = _L0_ffn_setup()
    _L0_ffn_in = {k: v for k, v in _L0_ffn_all.items() if k in ('gate_w', 'gate_up_proj', 'down_proj')}
    del _L0_ffn_all

    def _L1_xattn_setup():
        import jax, jax.numpy as jnp
        import numpy as np
        D_MODEL = 256
        NUM_HEADS = 16
        D_K = D_MODEL // NUM_HEADS
        NEG_INF = -1000000000.0

        def _split_heads(x):
            B, S, _ = x.shape
            return x.reshape(B, S, NUM_HEADS, D_K).transpose(0, 2, 1, 3)
        key = jax.random.key(seed)
        ks = jax.random.split(key, 12)
        B, S = (4, 512)
        s = 1.0 / np.sqrt(D_MODEL)
        inp = {'Q': jax.random.normal(ks[0], (B, S, D_MODEL), jnp.float32), 'K': jax.random.normal(ks[1], (B, S, D_MODEL), jnp.float32), 'V': jax.random.normal(ks[2], (B, S, D_MODEL), jnp.float32), 'mask': jnp.ones((B, S, S), jnp.int32), 'Wq': jax.random.normal(ks[3], (D_MODEL, D_MODEL), jnp.float32) * s, 'bq': jax.random.normal(ks[4], (D_MODEL,), jnp.float32) * s, 'Wk': jax.random.normal(ks[5], (D_MODEL, D_MODEL), jnp.float32) * s, 'bk': jax.random.normal(ks[6], (D_MODEL,), jnp.float32) * s, 'Wv': jax.random.normal(ks[7], (D_MODEL, D_MODEL), jnp.float32) * s, 'bv': jax.random.normal(ks[8], (D_MODEL,), jnp.float32) * s, 'Wo': jax.random.normal(ks[9], (D_MODEL, D_MODEL), jnp.float32) * s, 'bo': jax.random.normal(ks[10], (D_MODEL,), jnp.float32) * s}
        return inp
    _L1_xattn_all = _L1_xattn_setup()
    _L1_xattn_in = {k: v for k, v in _L1_xattn_all.items() if k in ('Wq', 'bq', 'Wk', 'bk', 'Wv', 'bv', 'Wo', 'bo')}
    del _L1_xattn_all

    def _L1_ffn_setup():
        import jax, jax.numpy as jnp
        import numpy as np
        B, T, DIM, H, DH, TOPK = (4, 512, 256, 8, 64, 3)
        key = jax.random.key(seed)
        ks = jax.random.split(key, 6)
        x = jax.random.normal(ks[0], (B, T, DIM), dtype=jnp.float32)
        sc = 1.0 / np.sqrt(DIM)
        Wq = jax.random.normal(ks[1], (DIM, H * DH), dtype=jnp.float32) * sc
        Wkv = jax.random.normal(ks[2], (DIM, 2 * H * DH), dtype=jnp.float32) * sc
        Ws = jax.random.normal(ks[3], (DIM, H), dtype=jnp.float32) * sc
        Wo = jax.random.normal(ks[4], (H, DH, DIM), dtype=jnp.float32) * (1.0 / np.sqrt(DH))
        bo = jax.random.normal(ks[5], (H, DIM), dtype=jnp.float32) * 0.01
        return {'x': x, 'Wq': Wq, 'Wkv': Wkv, 'Ws': Ws, 'Wo': Wo, 'bo': bo}
    _L1_ffn_all = _L1_ffn_setup()
    _L1_ffn_in = {k: v for k, v in _L1_ffn_all.items() if k in ('Wq', 'Wkv', 'Ws', 'Wo', 'bo')}
    del _L1_ffn_all
    return {'x': x, 'ctx_1024': ctx_1024, 'mask_BxSxS2_if1': mask_BxSxS2_if1, 'L0_ffn_gate_w': _L0_ffn_in['gate_w'], 'L0_ffn_gate_up_proj': _L0_ffn_in['gate_up_proj'], 'L0_ffn_down_proj': _L0_ffn_in['down_proj'], 'L1_xattn_Wq': _L1_xattn_in['Wq'], 'L1_xattn_bq': _L1_xattn_in['bq'], 'L1_xattn_Wk': _L1_xattn_in['Wk'], 'L1_xattn_bk': _L1_xattn_in['bk'], 'L1_xattn_Wv': _L1_xattn_in['Wv'], 'L1_xattn_bv': _L1_xattn_in['bv'], 'L1_xattn_Wo': _L1_xattn_in['Wo'], 'L1_xattn_bo': _L1_xattn_in['bo'], 'L1_ffn_Wq': _L1_ffn_in['Wq'], 'L1_ffn_Wkv': _L1_ffn_in['Wkv'], 'L1_ffn_Ws': _L1_ffn_in['Ws'], 'L1_ffn_Wo': _L1_ffn_in['Wo'], 'L1_ffn_bo': _L1_ffn_in['bo']}

def reference(x, ctx_1024, mask_BxSxS2_if1, L0_ffn_gate_w, L0_ffn_gate_up_proj, L0_ffn_down_proj, L1_xattn_Wq, L1_xattn_bq, L1_xattn_Wk, L1_xattn_bk, L1_xattn_Wv, L1_xattn_bv, L1_xattn_Wo, L1_xattn_bo, L1_ffn_Wq, L1_ffn_Wkv, L1_ffn_Ws, L1_ffn_Wo, L1_ffn_bo):
    import jax
    import jax.numpy as jnp

    def _L0_xattn_ref(query, keys, values):
        import jax, jax.numpy as jnp
        import numpy as np
        EMBED_SIZE = 256
        B, S, E = (8, 1024, EMBED_SIZE)

        def _feature_map(x):
            return jax.nn.gelu(x, approximate=False) + 1.0
        scaling = EMBED_SIZE ** 0.5
        q = _feature_map(query)
        k = _feature_map(keys)
        energy = jnp.sum(q * k, axis=1, keepdims=True) * q / scaling
        attention = jax.nn.softmax(energy, axis=1) * values
        return attention

    def _L0_ffn_ref(hidden_states, gate_w, gate_up_proj, down_proj):
        import jax, jax.numpy as jnp
        import numpy as np
        TOP_K = 2
        B, S, H = hidden_states.shape
        E = gate_w.shape[0]
        x = hidden_states.reshape(-1, H)
        T = x.shape[0]
        probs = jax.nn.softmax(x @ gate_w.T, axis=-1)
        w, idx = jax.lax.top_k(probs, TOP_K)
        w = w / jnp.sum(w, axis=-1, keepdims=True)
        combine = jnp.zeros((T, E), x.dtype).at[jnp.arange(T)[:, None], idx].add(w)

        def step(acc, inputs):
            gup, dn, ce = inputs
            g, u = jnp.split(x @ gup.T, 2, axis=-1)
            acc = acc + ce[:, None] * (jax.nn.silu(g) * u @ dn.T)
            return (acc, None)
        out, _ = jax.lax.scan(step, jnp.zeros_like(x), (gate_up_proj, down_proj, combine.T))
        return out.reshape(B, S, H)

    def _L1_xattn_ref(Q, K, V, mask, Wq, bq, Wk, bk, Wv, bv, Wo, bo):
        import jax, jax.numpy as jnp
        import numpy as np
        D_MODEL = 256
        NUM_HEADS = 16
        D_K = D_MODEL // NUM_HEADS
        NEG_INF = -1000000000.0

        def _split_heads(x):
            B, S, _ = x.shape
            return x.reshape(B, S, NUM_HEADS, D_K).transpose(0, 2, 1, 3)
        q = _split_heads(Q @ Wq.T + bq)
        k = _split_heads(K @ Wk.T + bk)
        v = _split_heads(V @ Wv.T + bv)
        scores = jnp.einsum('bhqd,bhkd->bhqk', q, k) / jnp.sqrt(jnp.float32(D_K))
        scores = jnp.where(mask[:, None, :, :] == 0, NEG_INF, scores)
        attn = jax.nn.softmax(scores, axis=-1)
        out = jnp.einsum('bhqk,bhkd->bhqd', attn, v)
        B, H, S, dk = out.shape
        out = out.transpose(0, 2, 1, 3).reshape(B, S, H * dk)
        return out @ Wo.T + bo

    def _L1_ffn_ref(x, Wq, Wkv, Ws, Wo, bo):
        import jax, jax.numpy as jnp
        import numpy as np
        B, T, DIM, H, DH, TOPK = (4, 512, 256, 8, 64, 3)
        b, t, _ = x.shape
        s = jax.nn.sigmoid(x @ Ws)
        vals, idx = jax.lax.top_k(s, TOPK)
        bi = jnp.arange(b)[:, None, None]
        ti = jnp.arange(t)[None, :, None]
        scores = jnp.zeros_like(s).at[bi, ti, idx].set(vals)
        q = (x @ Wq).reshape(b, t, H, DH).transpose(0, 2, 1, 3)
        kv = (x @ Wkv).reshape(b, t, 2, H, DH).transpose(2, 0, 3, 1, 4)
        k, v = (kv[0], kv[1])
        scale = DH ** (-0.5)
        attn = jax.nn.softmax(jnp.einsum('bhid,bhjd->bhij', q * scale, k), axis=-1)
        out = jnp.einsum('bhij,bhjd->bhid', attn, v)
        proj = jnp.einsum('bhtd,hde->bhte', out, Wo) + bo[None, :, None, :]
        return jnp.einsum('bhte,bth->bte', proj, scores)
    x = x + _L0_xattn_ref(_layernorm(x, axis=-1), ctx_1024, ctx_1024)
    x = x + _L0_ffn_ref(_layernorm(x, axis=-1), L0_ffn_gate_w, L0_ffn_gate_up_proj, L0_ffn_down_proj)
    x = x + _L1_xattn_ref(_layernorm(x, axis=-1), ctx_1024, ctx_1024, mask_BxSxS2_if1, L1_xattn_Wq, L1_xattn_bq, L1_xattn_Wk, L1_xattn_bk, L1_xattn_Wv, L1_xattn_bv, L1_xattn_Wo, L1_xattn_bo)
    x = x + _L1_ffn_ref(_layernorm(x, axis=-1), L1_ffn_Wq, L1_ffn_Wkv, L1_ffn_Ws, L1_ffn_Wo, L1_ffn_bo)
    return x

_drawn_inputs = setup_inputs


def setup_inputs(seed=0):
    import zlib

    import numpy as np

    out = dict(_drawn_inputs(seed))
    spreads = {}
    factors = {'L1_xattn_bk': 8.0, 'L1_ffn_bo': 5.744}
    for name, (base, spread) in spreads.items():
        noise = np.random.default_rng([zlib.crc32(name.encode()), seed]).standard_normal(out[name].shape)
        drawn = base * np.exp(spread * noise) if base else spread * noise
        out[name] = jnp.asarray(drawn.astype(out[name].dtype))
    for name, factor in factors.items():
        out[name] = (out[name] * factor).astype(out[name].dtype)
    return out
```

```python
from contextlib import ExitStack

import concourse.bass as bass
from concourse import mybir

ALU = mybir.AluOpType
ACT = mybir.ActivationFunctionType
AX = mybir.AxisListType
F32 = mybir.dt.float32
BF16 = mybir.dt.bfloat16
F32R = mybir.dt.float32r
I32 = mybir.dt.int32
U32 = mybir.dt.uint32

P = 128
B, S, D = 8, 512, 256
KC = D // P
TB = S // P
NT = B * TB
E, F = 8, 1024
FC = F // P
TOPK = 2
MAXT = NT * TOPK + E - 1
EPS = 1e-5
HEADS, DK = 16, 16
G, HG = 4, 4
SH, SDK, STOP = 8, 64, 3
MASKED = -2.0 ** 32


class Names:

    def __init__(self, nc, ctx, tag):
        self.nc, self.ctx, self.tag = nc, ctx, tag

    def sb(self, name, shape, dt=F32):
        return self.ctx.enter_context(self.nc.sbuf_tensor(f"{self.tag}_{name}", shape, dt))

    def ps(self, name, shape, dt=F32):
        return self.ctx.enter_context(self.nc.psum_tensor(f"{self.tag}_{name}", shape, dt))

    def sem(self, name):
        return self.ctx.enter_context(self.nc.semaphore(f"{self.tag}_{name}"))


def constants(nc, ident, before, ones, iota8):
    with ExitStack() as ctx:
        m = Names(nc, ctx, "const")
        filled, done = m.sem("filled"), m.sem("done")
        block = ctx.enter_context(nc.Block())

        @block.gpsimd
        def _(pool):
            pool.memset(ident[:, :], 0.0).then_inc(filled, 1)
            pool.memset(before[:, :], 0.0).then_inc(filled, 1)
            pool.memset(ones[:, :], 1.0).then_inc(done, 1)
            for e in range(E):
                pool.memset(iota8[:, e:e + 1], float(e)).then_inc(done, 1)
            pool.wait_ge(filled, 2)
            pool.affine_select(out=ident[:, :], in_=ident[:, :], compare_op=ALU.not_equal, fill=1.0,
                               base=0, pattern=[[-1, P]], channel_multiplier=1).then_inc(done, 1)
            pool.affine_select(out=before[:, :], in_=before[:, :], compare_op=ALU.is_ge, fill=1.0,
                               base=0, pattern=[[-1, P]], channel_multiplier=1).then_inc(done, 1)
            pool.wait_ge(done, E + 3)


def rstd_steps(act, dve, *, var, std, rstd, eps, stats_ready, std_ready, rstd_ready):
    if act is not None:
        act.wait_ge(stats_ready, 1)
        act.activation(std, var, ACT.Sqrt, bias=eps).then_inc(std_ready, 1)
    if dve is not None:
        dve.wait_ge(std_ready, 1)
        dve.reciprocal(rstd, std).then_inc(rstd_ready, 1)


def feature_attention(nc, x_in, ctxT_in, x, stats, ident):
    with ExitStack() as ctx:
        m = Names(nc, ctx, "fa")
        st6 = m.sb("st6", [P, NT, 6])
        mv = m.sb("mv", [P, NT, 2])
        std = m.sb("std", [P, NT])
        rstd = m.sb("rstd", [P, NT])
        eps = m.sb("eps", [P, 1])
        ctxT = m.sb("ctxT", [P, KC, B * S])
        gq = m.sb("gq", [P, KC, B * S])
        xn = m.sb("xn", [P, TB, D])
        gk = m.sb("gk", [P, KC, S])
        k1 = m.sb("k1", [P, KC, S])
        junk = m.sb("junk", [P, KC, S])
        qk = m.sb("qk", [P, KC, 1])
        ex = m.sb("ex", [P, KC, S])
        at = m.sb("at", [P, KC, S])
        negmax = m.sb("negmax", [P, KC * B])
        esum = m.sb("esum", [P, KC])
        rsum = m.sb("rsum", [P, KC])
        xnT = m.ps("xnT", [P, KC, S])
        att = m.ps("att", [P, TB, D])

        x_in_done = [m.sem(f"x_in{i}") for i in range(4)]
        ctx_in = m.sem("ctx_in")
        eps_set = m.sem("eps_set")
        st_done = m.sem("st_done")
        stats_ready, std_ready, rstd_ready = m.sem("stats_ready"), m.sem("std_ready"), m.sem("rstd_ready")
        xn_ready, xnT_ready = m.sem("xn_ready"), m.sem("xnT_ready")
        gq_ready, gk_ready, k1_ready = m.sem("gq_ready"), m.sem("gk_ready"), m.sem("k1_ready")
        qk_ready, qks_ready, en_ready = m.sem("qk_ready"), m.sem("qks_ready"), m.sem("en_ready")
        mx_ready = m.sem("mx_ready")
        ex_ready, rs_ready, at_ready, att_ready = m.sem("ex_ready"), m.sem("rs_ready"), m.sem("at_ready"), m.sem("att_ready")
        x_added, st2_done = m.sem("x_added"), m.sem("st2_done")
        block = ctx.enter_context(nc.Block())
        xv = x_in.rearrange("(t p) d -> p t d", p=P)

        @block.sync
        def _(sp):
            for i in range(4):
                sp.dma_start(x[:, i * TB * 2:(i + 1) * TB * 2, :], xv[:, i * TB * 2:(i + 1) * TB * 2, :]).then_inc(x_in_done[i], 16)
            sp.dma_start(ctxT[:, :, :], ctxT_in.rearrange("(c p) n -> p c n", p=P)).then_inc(ctx_in, 16)

        @block.tensor
        def _(pe):
            with pe.Fori(0, B) as b:
                pe.wait_ge(xn_ready, (b + 1) * TB)
                pe.wait_ge(gq_ready, b + 1)
                for i in range(TB):
                    for c in range(KC):
                        last = pe.transpose(xnT[:, c, i * P:(i + 1) * P], xn[:, i, c * P:(c + 1) * P], ident[:, :])
                last.then_inc(xnT_ready, 1)
            with pe.Fori(0, B) as b:
                pe.wait_ge(at_ready, (b + 1) * KC + 1)
                pe.wait_ge(x_added, b + 1)
                for i in range(TB):
                    for c in range(KC):
                        last = pe.transpose(att[:, i, c * P:(c + 1) * P], at[:, c, i * P:(i + 1) * P], ident[:, :])
                last.then_inc(att_ready, 1)

        @block.scalar
        def _(act):
            act.wait_ge(eps_set, 1)
            rstd_steps(act, None, var=mv[:, :, 1], std=std[:, :], rstd=None, eps=eps[:, 0:1],
                       stats_ready=stats_ready, std_ready=std_ready, rstd_ready=None)
            act.activation(junk[:, 0, 0:1], eps[:, 0:1], ACT.Gelu).then_inc(gq_ready, 1)
            act.wait_ge(ctx_in, 16)
            with act.Fori(0, B) as b:
                act.wait_ge(k1_ready, b + 1)
                act.activation(gk[:, :, :], ctxT[:, :, bass.ts(b, S)], ACT.Gelu).then_inc(gk_ready, 1)
                act.wait_ge(xnT_ready, b + 1)
                act.activation(gq[:, :, bass.ts(b, S)], xnT[:, :, :], ACT.Gelu).then_inc(gq_ready, 1)
            act.wait_ge(mx_ready, B)
            with act.Fori(0, B) as b:
                act.wait_ge(at_ready, b * KC + 1)
                for c in range(KC):
                    act.activation(ex[:, c, :], gq[:, c, bass.ts(b, S)], ACT.Exp,
                                   bias=negmax[:, bass.ds(b * KC + c, 1)], accum_out=esum[:, c:c + 1]).then_inc(ex_ready, 1)

        @block.vector
        def _(dve):
            dve.memset(eps[:, :], EPS).then_inc(eps_set, 1)
            for t in range(NT):
                if t % (TB * 2) == 0:
                    dve.wait_ge(x_in_done[t // (TB * 2)], 16)
                dve.bn_stats(st6[:, t, :], x[:, t, :]).then_inc(st_done, 1)
            for t in range(NT):
                if t in (0, NT // 2):
                    dve.wait_ge(st_done, NT)
                last = dve.bn_aggr(mv[:, t, :], st6[:, t, :])
            last.then_inc(stats_ready, 1)
            rstd_steps(None, dve, var=None, std=std[:, :], rstd=rstd[:, :], eps=None,
                       stats_ready=None, std_ready=std_ready, rstd_ready=rstd_ready)
            dve.wait_ge(rstd_ready, 1)
            dve.memset(k1[:, :, :], 0.0).then_inc(k1_ready, 1)
            with dve.Fori(0, B) as b:
                for i in range(TB):
                    dve.tensor_scalar(xn[:, i, :], x[:, bass.ds(b * TB + i, 1), :], mv[:, bass.ds(b * TB + i, 1), 0],
                                      rstd[:, bass.ds(b * TB + i, 1)], ALU.subtract, ALU.mult).then_inc(xn_ready, 1)
                dve.wait_ge(gk_ready, b + 1)
                dve.tensor_scalar(k1[:, :, :], gk[:, :, :], 1.0, None, ALU.add).then_inc(k1_ready, 1)
                dve.wait_ge(k1_ready, b + 2)
                dve.wait_ge(gq_ready, b + 2)
                for c in range(KC):
                    dve.scalar_tensor_tensor(out=junk[:, c, :], in0=gq[:, c, bass.ts(b, S)], scalar=1.0, in1=k1[:, c, :],
                                             op0=ALU.add, op1=ALU.mult, accum_out=qk[:, c, :]).then_inc(qk_ready, 1)
                dve.wait_ge(qk_ready, (b + 1) * KC)
                dve.tensor_scalar(qk[:, :, :], qk[:, :, :], 1.0 / D ** 0.5, None, ALU.mult).then_inc(qks_ready, 1)
                dve.wait_ge(qks_ready, b + 1)
                for c in range(KC):
                    dve.tensor_scalar(gq[:, c, bass.ts(b, S)], gq[:, c, bass.ts(b, S)], 1.0, qk[:, c, :],
                                      ALU.add, ALU.mult).then_inc(en_ready, 1)
                dve.wait_ge(en_ready, (b + 1) * KC)
                dve.tensor_reduce(negmax[:, bass.ds(b * KC, KC)], gq[:, :, bass.ts(b, S)], AX.X, ALU.max,
                                  negate=True).then_inc(mx_ready, 1)
            dve.memset(rsum[:, :], 0.0).then_inc(at_ready, 1)
            dve.wait_ge(at_ready, 1)
            dve.memset(junk[:, 0, 0:1], 0.0).then_inc(x_added, 1)
            with dve.Fori(0, B) as b:
                dve.wait_ge(ex_ready, (b + 1) * KC)
                dve.reciprocal(rsum[:, :], esum[:, :]).then_inc(rs_ready, 1)
                dve.wait_ge(rs_ready, b + 1)
                for c in range(KC):
                    dve.scalar_tensor_tensor(out=at[:, c, :], in0=ex[:, c, :], scalar=rsum[:, c:c + 1],
                                             in1=ctxT[:, c, bass.ts(b, S)], op0=ALU.mult, op1=ALU.mult).then_inc(at_ready, 1)
                dve.wait_ge(att_ready, b + 1)
                dve.tensor_tensor(x[:, bass.ts(b, TB), :], att[:, :, :], x[:, bass.ts(b, TB), :], ALU.add).then_inc(x_added, 1)
                dve.wait_ge(x_added, b + 2)
                for i in range(TB):
                    dve.bn_stats(stats[:, bass.ds(b * TB + i, 1), :], x[:, bass.ds(b * TB + i, 1), :]).then_inc(st2_done, 1)
            dve.wait_ge(st2_done, NT)


def route(nc, gateT_in, rows, outs, x, stats, ident, before, ones, iota8, xn, weight, place, tile_at):
    with ExitStack() as ctx:
        m = Names(nc, ctx, "rt")
        mv = m.sb("mv", [P, NT, 2])
        std, rstd, eps = m.sb("std", [P, NT]), m.sb("rstd", [P, NT]), m.sb("eps", [P, 1])
        zeros = m.sb("zeros", [P, 4 * D])
        gateT = m.sb("gateT", [P, KC, E])
        xt = m.sb("xt", [P, 2, KC, P])
        logit = m.sb("logit", [P, NT, E])
        top = m.sb("top", [P, NT, 8])
        topi = m.sb("topi", [P, NT, 8], U32)
        topf = m.sb("topf", [P, NT, 8])
        hot = m.sb("hot", [P, TOPK, NT, E])
        both = m.sb("both", [P, NT, E])
        scan = m.sb("scan", [P, 2, NT, E])
        counts = m.sb("counts", [P, E])
        tiles_i = m.sb("tiles_i", [P, E], I32)
        tiles_f = m.sb("tiles_f", [P, E])
        start = m.sb("start", [P, E + 1])
        pos = m.sb("pos", [P, NT, E])
        picked = m.sb("picked", [P, TOPK, NT, E])
        placef = m.sb("placef", [P, TOPK, NT])
        wtmp = m.sb("wtmp", [P, 3, NT])
        xtp = [m.ps(f"xtp{i}", [P, KC, P]) for i in range(2)]
        lg = m.ps("lg", [P, NT, E])
        inside = m.ps("inside", [P, NT, E])
        total = m.ps("total", [P, NT, E])

        gate_in, zero_set, zeroed = m.sem("gate_in"), m.sem("zero_set"), m.sem("zeroed")
        aggr, eps_set, stats_ready, std_ready, rstd_ready = (m.sem("aggr"), m.sem("eps_set"), m.sem("stats_ready"),
                                                             m.sem("std_ready"), m.sem("rstd_ready"))
        xn_ready, xtp_ready, xt_ready, lg_ready, lg_out = (m.sem("xn_ready"), m.sem("xtp_ready"), m.sem("xt_ready"),
                                                           m.sem("lg_ready"), m.sem("lg_out"))
        both_ready, sums_ready, diff_ready, exp_ready, placed, scattered = (
            m.sem("both_ready"), m.sem("sums_ready"), m.sem("diff_ready"), m.sem("exp_ready"), m.sem("placed"), m.sem("scattered"))
        step, spare_zeroed = m.sem("step"), m.sem("spare_zeroed")
        block = ctx.enter_context(nc.Block())

        @block.sync
        def _(sp):
            sp.dma_start(gateT[:, :, :], gateT_in.rearrange("(c p) e -> p c e", p=P)).then_inc(gate_in, 16)
            sp.wait_ge(zero_set, 1)
            per = rows.shape[0] // (4 * P)
            for i in range(per):
                sp.dma_start(rows[i * 4 * P:(i + 1) * 4 * P, :].rearrange("(p r) d -> p (r d)", p=P), zeros[:, :]).then_inc(zeroed, 16)
            sp.dma_start(outs[NT * TOPK * P:MAXT * P, :].rearrange("(p r) d -> p r d", p=P), 
                         zeros[:, 0:D].rearrange("p (a d) -> p a d", a=1).to_broadcast([P, MAXT - NT * TOPK, D])).then_inc(spare_zeroed, 16)
            sp.wait_ge(zeroed, 16 * per)
            sp.wait_ge(spare_zeroed, 16)

        def gate_tile(pe, t):
            pe.wait_ge(xt_ready, t + 1)
            for c in range(KC):
                last = pe.matmul(lg[:, t, :], xt[:, t % 2, c, :], gateT[:, c, :], start=(c == 0), stop=(c == KC - 1))
            last.then_inc(lg_ready, 1)

        @block.tensor
        def _(pe):
            pe.wait_ge(gate_in, 16)
            for t in range(NT):
                pe.wait_ge(xn_ready, t + 1)
                if t >= 2:
                    pe.wait_ge(xt_ready, t - 1)
                for c in range(KC):
                    last = pe.transpose(xtp[t % 2][:, c, :], xn[:, t, c * P:(c + 1) * P], ident[:, :])
                last.then_inc(xtp_ready, 1)
                if t >= 1:
                    gate_tile(pe, t - 1)
            gate_tile(pe, NT - 1)
            pe.wait_ge(both_ready, 1)
            pe.matmul(inside[:, :, :], before[:, :], both[:, :, :], start=True, stop=True).then_inc(sums_ready, 1)
            pe.matmul(total[:, :, :], ones[:, :], both[:, :, :], start=True, stop=True).then_inc(sums_ready, 1)

        @block.scalar
        def _(act):
            act.wait_ge(eps_set, 1)
            rstd_steps(act, None, var=mv[:, :, 1], std=std[:, :], rstd=None, eps=eps[:, 0:1],
                       stats_ready=stats_ready, std_ready=std_ready, rstd_ready=None)
            for t in range(NT):
                act.wait_ge(xtp_ready, t + 1)
                if t >= 2:
                    act.wait_ge(lg_ready, t - 1)
                act.copy(xt[:, t % 2, :, :], xtp[t % 2][:, :, :]).then_inc(xt_ready, 1)
            act.wait_ge(diff_ready, 1)
            act.activation(wtmp[:, 1, :], wtmp[:, 0, :], ACT.Exp).then_inc(exp_ready, 1)

        @block.gpsimd
        def _(pool):
            pool.memset(zeros[:, :], 0.0).then_inc(zero_set, 1)
            pool.wait_ge(placed, 1)
            pool.wait_ge(zeroed, 16 * (rows.shape[0] // (4 * P)))
            for t in range(NT):
                for j in range(TOPK):
                    pool.indirect_dma_start(rows, bass.IndirectOffsetOnAxis(ap=place[:, j, t:t + 1], axis=0),
                                            xn[:, t, :], None).then_inc(scattered, 16)
            pool.wait_ge(scattered, 16 * NT * TOPK)

        @block.vector
        def _(dve):
            n = [0]

            def then(ins):
                n[0] += 1
                ins.then_inc(step, 1)
                dve.wait_ge(step, n[0])

            dve.memset(eps[:, :], EPS).then_inc(eps_set, 1)
            for t in range(NT):
                last = dve.bn_aggr(mv[:, t, :], stats[:, t, :])
            last.then_inc(stats_ready, 1)
            rstd_steps(None, dve, var=None, std=std[:, :], rstd=rstd[:, :], eps=None,
                       stats_ready=None, std_ready=std_ready, rstd_ready=rstd_ready)
            dve.wait_ge(rstd_ready, 1)
            for t in range(NT):
                dve.tensor_scalar(xn[:, t, :], x[:, t, :], mv[:, t, 0:1], rstd[:, t:t + 1],
                                  ALU.subtract, ALU.mult).then_inc(xn_ready, 1)
            dve.wait_ge(lg_ready, NT)
            dve.tensor_copy(logit[:, :, :], lg[:, :, :]).then_inc(lg_out, 1)
            dve.wait_ge(lg_out, 1)
            for t in range(NT):
                last = dve.max(top[:, t, :], logit[:, t, :])
            then(last)
            for t in range(NT):
                last = dve.max_index(topi[:, t, :], top[:, t, :], logit[:, t, :])
            then(last)
            then(dve.tensor_copy(topf[:, :, :], topi[:, :, :]))
            experts = iota8[:, :].rearrange("p (a e) -> p a e", a=1).to_broadcast([P, NT, E])
            for j in range(TOPK):
                ins = dve.tensor_tensor(hot[:, j, :, :], topf[:, :, j:j + 1].to_broadcast([P, NT, E]), experts, ALU.is_equal)
            then(ins)
            dve.tensor_tensor(both[:, :, :], hot[:, 0, :, :], hot[:, 1, :, :], ALU.add).then_inc(both_ready, 1)
            dve.tensor_tensor(wtmp[:, 0, :], top[:, :, 1], top[:, :, 0], ALU.subtract).then_inc(diff_ready, 1)
            dve.wait_ge(exp_ready, 1)
            then(dve.tensor_scalar(wtmp[:, 2, :], wtmp[:, 1, :], 1.0, None, ALU.add))
            then(dve.reciprocal(weight[:, 0, :], wtmp[:, 2, :]))
            then(dve.tensor_tensor(weight[:, 1, :], wtmp[:, 1, :], weight[:, 0, :], ALU.mult))
            dve.wait_ge(sums_ready, 2)
            dve.memset(scan[:, 0, 0:1, :], 0.0)
            then(dve.tensor_copy(scan[:, 0, 1:NT, :], total[:, 0:NT - 1, :]))
            src, d = 0, 1
            while d < NT:
                dve.tensor_copy(scan[:, 1 - src, 0:d, :], scan[:, src, 0:d, :])
                then(dve.tensor_tensor(scan[:, 1 - src, d:NT, :], scan[:, src, d:NT, :], scan[:, src, 0:NT - d, :], ALU.add))
                src, d = 1 - src, 2 * d
            then(dve.tensor_tensor(counts[:, :], total[:, NT - 1, :], scan[:, src, NT - 1, :], ALU.add))
            then(dve.tensor_scalar(counts[:, :], counts[:, :], 1.0, float(P - 1), ALU.max, ALU.add))
            then(dve.tensor_copy(tiles_i[:, :], counts[:, :]))
            then(dve.tensor_scalar(tiles_i[:, :], tiles_i[:, :], 7, None, ALU.arith_shift_right))
            then(dve.tensor_copy(tiles_f[:, :], tiles_i[:, :]))
            then(dve.memset(start[:, 0:1], 0.0))
            for e in range(E):
                then(dve.tensor_tensor(start[:, e + 1:e + 2], start[:, e:e + 1], tiles_f[:, e:e + 1], ALU.add))
            dve.tensor_copy(tile_at[:, :], start[:, :])
            then(dve.tensor_tensor(pos[:, :, :], inside[:, :, :], scan[:, src, :, :], ALU.add))
            then(dve.tensor_scalar(start[:, :], start[:, :], float(P), None, ALU.mult))
            first = start[:, 0:E].rearrange("p (a e) -> p a e", a=1).to_broadcast([P, NT, E])
            then(dve.tensor_tensor(pos[:, :, :], pos[:, :, :], first, ALU.add))
            for j in range(TOPK):
                ins = dve.tensor_tensor(picked[:, j, :, :], hot[:, j, :, :], pos[:, :, :], ALU.mult)
            then(ins)
            then(dve.tensor_reduce(placef[:, :, :], picked[:, :, :, :], AX.X, ALU.add))
            dve.tensor_copy(place[:, :, :], placef[:, :, :]).then_inc(placed, 1)


def experts(nc, gateupT_in, downT_in, rows, outs, ident, tile_at):
    with ExitStack() as ctx:
        m = Names(nc, ctx, "ex")
        gu_w = [m.sb(f"gu_w{i}", [P, KC, 2 * F]) for i in range(2)]
        dn_w = [m.sb(f"dn_w{i}", [P, FC, D]) for i in range(2)]
        xin = m.sb("xin", [P, D])
        xt = m.sb("xt", [P, KC, P])
        sg = m.sb("sg", [P, 2, FC // 2, P])
        h = m.sb("h", [P, FC, P])
        y = m.sb("y", [P, D])
        xtp = m.ps("xtp", [P, KC, P])
        gp = [m.ps(f"gp{i}", [P, FC // 2, P]) for i in range(2)]
        up = [m.ps(f"up{i}", [P, FC // 2, P]) for i in range(2)]
        yp = m.ps("yp", [P, D])
        mark = m.ps("mark", [P, P])
        expert_done = m.sem("expert_done")
        w_in = [m.sem(f"w_in{i}") for i in range(2)]
        x_in, xtp_ready, xt_ready, g_ready, s_ready, u_ready, h_ready, yp_ready, y_ready, stored = (
            m.sem(n) for n in ("x_in", "xtp_ready", "xt_ready", "g_ready", "s_ready", "u_ready", "h_ready", "yp_ready", "y_ready", "stored"))
        block = ctx.enter_context(nc.Block())
        HC = FC // 2

        def bound(eng, e):
            return eng.value_load(tile_at[0:1, e:e + 1], min_val=1 if e else 0, max_val=MAXT)

        @block.sync
        def _(sp):
            total = bound(sp, E)
            with sp.Fori(0, sp.snap(total + 1)) as g:
                sp.wait_ge(xtp_ready, g + 1)
                sp.dma_start(xin[:, :], rows[bass.ts(g, P), :]).then_inc(x_in, 16)

        @block.gpsimd
        def _(pool):
            for e in range(E):
                if e >= 2:
                    pool.wait_ge(expert_done, e - 1)
                pool.dma_start(gu_w[e % 2][:, :, :], gateupT_in[e].rearrange("(c p) f -> p c f", p=P)).then_inc(w_in[e % 2], 16)
                pool.dma_start(dn_w[e % 2][:, :, :], downT_in[e].rearrange("(c p) d -> p c d", p=P)).then_inc(w_in[e % 2], 16)

        @block.tensor
        def _(pe):
            def turn():
                for c in range(KC):
                    last = pe.transpose(xtp[:, c, :], xin[:, c * P:(c + 1) * P], ident[:, :])
                last.then_inc(xtp_ready, 1)

            pe.transpose(xtp[:, 0, :], ident[:, :], ident[:, :]).then_inc(xtp_ready, 1)
            pe.wait_ge(x_in, 16)
            turn()
            for e in range(E):
                pe.wait_ge(w_in[e % 2], 32 * (e // 2 + 1))
                with pe.Fori(bound(pe, e), bound(pe, e + 1)) as g:
                    pe.wait_ge(xt_ready, g + 1)
                    for i in range(2):
                        for w, out, done in ((0, gp[i], g_ready), (F, up[i], u_ready)):
                            for f in range(HC):
                                col = w + (i * HC + f) * P
                                for c in range(KC):
                                    last = pe.matmul(out[:, f, :], gu_w[e % 2][:, c, col:col + P], xt[:, c, :],
                                                     start=(c == 0), stop=(c == KC - 1))
                            last.then_inc(done, 1)
                    pe.wait_ge(x_in, g * 16 + 32)
                    turn()
                    pe.wait_ge(y_ready, g + 1)
                    for i in range(2):
                        pe.wait_ge(h_ready, 2 * g + i + 1)
                        for f in range(i * HC, (i + 1) * HC):
                            last = pe.matmul(yp[:, :], h[:, f, :], dn_w[e % 2][:, f, :], start=(f == 0), stop=(f == FC - 1))
                    last.then_inc(yp_ready, 1)
                pe.transpose(mark[:, :], ident[:, :], ident[:, :]).then_inc(expert_done, 1)

        @block.scalar
        def _(act):
            act.copy(y[:, 0:1], ident[:, 0:1]).then_inc(y_ready, 1)
            act.wait_ge(y_ready, 1)
            with act.Fori(0, bound(act, E)) as g:
                for i in range(2):
                    act.wait_ge(g_ready, 2 * g + i + 1)
                    act.activation(sg[:, i, :, :], gp[i][:, :, :], ACT.Silu).then_inc(s_ready, 1)
                act.wait_ge(yp_ready, g + 1)
                act.copy(y[:, :], yp[:, :]).then_inc(y_ready, 1)
                act.wait_ge(y_ready, g + 2)
                act.dma_start(outs[bass.ts(g, P), :], y[:, :]).then_inc(stored, 16)
                act.wait_ge(stored, g * 16 + 16)

        @block.vector
        def _(dve):
            dve.wait_ge(xtp_ready, 2)
            dve.tensor_copy(xt[:, :, :], xtp[:, :, :]).then_inc(xt_ready, 1)
            with dve.Fori(0, bound(dve, E)) as g:
                for i in range(2):
                    dve.wait_ge(u_ready, 2 * g + i + 1)
                    dve.wait_ge(s_ready, 2 * g + i + 1)
                    dve.tensor_tensor(h[:, i * HC:(i + 1) * HC, :], up[i][:, :, :], sg[:, i, :, :], ALU.mult).then_inc(h_ready, 1)
                dve.wait_ge(xtp_ready, g + 3)
                dve.tensor_copy(xt[:, :, :], xtp[:, :, :]).then_inc(xt_ready, 1)


def combine(nc, outs, x, weight, place):
    with ExitStack() as ctx:
        m = Names(nc, ctx, "cb")
        got = m.sb("got", [P, NT, TOPK, D])
        gathered = [m.sem(f"gathered{i}") for i in range(4)]
        added = m.sem("added")
        block = ctx.enter_context(nc.Block())
        G = NT // 4

        @block.gpsimd
        def _(pool):
            for t in range(NT):
                for j in range(TOPK):
                    pool.indirect_dma_start(got[:, t, j, :], None, outs,
                                            bass.IndirectOffsetOnAxis(ap=place[:, j, t:t + 1], axis=0)).then_inc(gathered[t // G], 16)

        @block.vector
        def _(dve):
            for t in range(NT):
                if t % G == 0:
                    dve.wait_ge(gathered[t // G], 16 * G * TOPK)
                dve.scalar_tensor_tensor(out=x[:, t, :], in0=got[:, t, 0, :], scalar=weight[:, 0, t:t + 1],
                                         in1=x[:, t, :], op0=ALU.mult, op1=ALU.add).then_inc(added, 1)
            for t in range(NT):
                dve.wait_ge(added, t + 1)
                dve.scalar_tensor_tensor(out=x[:, t, :], in0=got[:, t, 1, :], scalar=weight[:, 1, t:t + 1],
                                         in1=x[:, t, :], op0=ALU.mult, op1=ALU.add).then_inc(added, 1)
            dve.wait_ge(added, 2 * NT)



def masks(nc, mask_in, maskT_in, bias, biasT, flag, ones):
    with ExitStack() as ctx:
        m = Names(nc, ctx, "mk")
        raw = [m.sb(f"raw{i}", [P, TB, S], I32) for i in range(2)]
        out = [m.sb(f"out{i}", [P, TB, S], BF16) for i in range(2)]
        least = m.sb("least", [P, B, TB])
        lowest = m.sb("lowest", [P, 1])
        summed = m.ps("summed", [P, 1])
        raw_in = [m.sem(f"raw_in{i}") for i in range(2)]
        made = [m.sem(f"made{i}") for i in range(2)]
        stored = [m.sem(f"stored{i}") for i in range(2)]
        least_ready, lowest_ready, summed_ready, flag_ready = (m.sem(n) for n in ("least_ready", "lowest_ready", "summed_ready", "flag_ready"))
        block = ctx.enter_context(nc.Block())
        src, dst = (mask_in, maskT_in), (bias, biasT)

        @block.sync
        def _(sp):
            with sp.Fori(0, B) as b:
                for i in range(2):
                    sp.wait_ge(made[i], b + 1)
                    sp.dma_start(raw[i][:, :, :], src[i][bass.ds(b * S, S), :].rearrange("(t p) n -> p t n", p=P)).then_inc(raw_in[i], 16)

        @block.gpsimd
        def _(pool):
            for i in range(2):
                pool.memset(out[i][:, 0, :], 0.0).then_inc(made[i], 1)

        @block.vector
        def _(dve):
            dve.wait_ge(made[0], 1)
            dve.wait_ge(made[1], 1)
            with dve.Fori(0, B) as b:
                for i in range(2):
                    dve.wait_ge(raw_in[i], b * 16 + 16)
                    dve.wait_ge(stored[i], b * 16 + 16)
                    dve.tensor_scalar(out[i][:, :, :], raw[i][:, :, :], 0.0, MASKED, ALU.is_equal, ALU.mult).then_inc(made[i], 1)
                dve.wait_ge(made[0], b + 2)
                dve.tensor_reduce(least[:, bass.ds(b, 1), :], out[0][:, :, :], AX.X, ALU.min).then_inc(least_ready, 1)
                dve.wait_ge(least_ready, b + 1)
            dve.wait_ge(least_ready, B)
            dve.tensor_reduce(lowest[:, :], least[:, :, :], AX.XY, ALU.min).then_inc(lowest_ready, 1)
            dve.wait_ge(summed_ready, 1)
            dve.tensor_scalar(flag[:, :], summed[:, :], 0.0, None, ALU.is_lt).then_inc(flag_ready, 1)

        @block.tensor
        def _(pe):
            pe.wait_ge(lowest_ready, 1)
            pe.matmul(summed[:, :], ones[:, :], lowest[:, :], start=True, stop=True).then_inc(summed_ready, 1)

        @block.scalar
        def _(act):
            act.wait_ge(made[0], 1)
            act.wait_ge(made[1], 1)
            for i in range(2):
                act.dma_start(dst[i][0:P, :], out[i][:, 0, :]).then_inc(stored[i], 16)
            with act.Fori(0, B) as b:
                for i in range(2):
                    act.wait_ge(made[i], b + 2)
                    act.dma_start(dst[i][bass.ds(b * S, S), :].rearrange("(t p) n -> p t n", p=P), out[i][:, :, :]).then_inc(stored[i], 16)
            for i in range(2):
                act.wait_ge(stored[i], 16 * (B + 1))


def norm_stats(nc, x, mv, rstd, tag):
    with ExitStack() as ctx:
        m = Names(nc, ctx, tag)
        st6, std, eps = m.sb("st6", [P, NT, 6]), m.sb("std", [P, NT]), m.sb("eps", [P, 1])
        st_ready, stats_ready, std_ready, rstd_ready, eps_set = (m.sem(n) for n in ("st_ready", "stats_ready", "std_ready", "rstd_ready", "eps_set"))
        block = ctx.enter_context(nc.Block())

        @block.scalar
        def _(act):
            act.wait_ge(eps_set, 1)
            rstd_steps(act, None, var=mv[:, :, 1], std=std[:, :], rstd=None, eps=eps[:, 0:1],
                       stats_ready=stats_ready, std_ready=std_ready, rstd_ready=None)

        @block.vector
        def _(dve):
            dve.memset(eps[:, :], EPS).then_inc(eps_set, 1)
            for t in range(NT):
                dve.bn_stats(st6[:, t, :], x[:, t, :]).then_inc(st_ready, 1)
            dve.wait_ge(st_ready, NT)
            for t in range(NT):
                last = dve.bn_aggr(mv[:, t, :], st6[:, t, :])
            last.then_inc(stats_ready, 1)
            rstd_steps(None, dve, var=None, std=std[:, :], rstd=rstd[:, :], eps=None,
                       stats_ready=None, std_ready=std_ready, rstd_ready=rstd_ready)
            dve.wait_ge(rstd_ready, 1)


def cross_attention(nc, io, x, mv, rstd, ident, ones, bias, biasT, flag, q_parts, k_parts):
    with ExitStack() as ctx:
        m = Names(nc, ctx, "ca")
        R4 = 4 * DK
        wq, wk, wv = (m.sb(n, [P, KC, D]) for n in ("wq", "wk", "wv"))
        wo = m.sb("wo", [P, G, D])
        bq, bk, bv = m.sb("bq", [P, KC]), m.sb("bk", [P, KC]), m.sb("bv", [P, D])
        ident16, tiny16 = m.sb("ident16", [P, P], BF16), m.sb("tiny16", [P, P], BF16)
        xn, xT = m.sb("xn", [P, TB, D]), m.sb("xT", [P, KC, S])
        ctxT = m.sb("ctxT", [P, KC, S])
        nb, nbT = m.sb("nb", [P, 2, TB, S], BF16), m.sb("nbT", [P, 2, TB, S], BF16)
        rv = m.sb("rv", [P, S])
        qf = m.sb("qf", [P, KC, S])
        qp, kp = m.sb("qp", [P, 2, KC, S], F32R), m.sb("kp", [P, 2, KC, S], F32R)
        q_stack = [m.sb(f"q_stack{g}", [P, HG, S], F32R) for g in range(G)]
        k_stack = [m.sb(f"k_stack{g}", [P, HG, S], F32R) for g in range(G)]
        negmax = m.sb("negmax", [P, 2, TB, HG])
        zrow = m.sb("zrow", [2, S])
        mrow = m.sb("mrow", [HG, 2, S], F32R)
        pr = m.sb("pr", [P, 2, HG, S])
        vstage = m.sb("vstage", [P, TB, D])
        vw = m.sb("vw", [P, G, TB, HG, 32])
        sums, rec = m.sb("sums", [P, S]), m.sb("rec", [P, S])
        outT = m.sb("outT", [P, G, S])
        tick = m.sb("tick", [P, 1])
        na = [m.ps(f"na{i}", [P, S]) for i in range(2)]
        st = [m.ps(f"st{i}", [P, 2, S]) for i in range(2)]
        av, misc = m.ps("av", [P, S]), m.ps("misc", [P, S])

        w_in, set_up = m.sem("w_in"), m.sem("set_up")
        ctx_in, nb_in, nbT_in = m.sem("ctx_in"), m.sem("nb_in"), m.sem("nbT_in")
        xn_ready = m.sem("xn_ready")
        qp_ready = m.sem("qp_ready")
        k_head, q_head = m.sem("k_head"), m.sem("q_head")
        k_stored, q_stored = m.sem("k_stored"), m.sem("q_stored")
        stack_in = [m.sem(f"stack_in{g}") for g in range(G)]
        na_full, max_done, st_full, exp_done = m.sem("na_full"), m.sem("max_done"), m.sem("st_full"), m.sem("exp_done")
        mh_ready, m_in = m.sem("mh_ready"), m.sem("m_in")
        av_done, vw_ready = m.sem("av_done"), m.sem("vw_ready")
        sums_ready, rec_ready, outT_ready = m.sem("sums_ready"), m.sem("rec_ready"), m.sem("outT_ready")
        misc_full, misc_free = m.sem("misc_full"), m.sem("misc_free")
        block = ctx.enter_context(nc.Block())

        SETUP = 7 + 2 * G
        LOAD = 16 * 9
        SLOTS = TB * HG
        JOBS = [("m", 0, 1), ("k0", 0, 3), ("k1", 0, 5), ("xT0", 0, 6), ("xT1", 0, 8), ("rv", 0, 9),
                ("q0", 0, 11), ("q1", 0, 13), ("o0", 0, 15), ("o1", 1, 0), ("m", 1, 2), ("v0", 1, 5),
                ("v1", 1, 8), ("m", 2, 1), ("m", 3, 1)]
        FIRST = ["k0", "k1", "xT0", "xT1", "rv", "q0", "q1", "v0", "v1", "m"]
        nj, nf = len(JOBS), len(FIRST)

        def jobs_at(g, s):
            return [(n, j[0]) for n, j in enumerate(JOBS) if j[1:] == (g, s)]

        def number(name):
            return next(n for n, j in enumerate(JOBS) if j[0] == name)

        def nxt(b):
            return b + 1 if isinstance(b, int) else (b + 1) % B

        @block.sync
        def _(sp):
            def load_ctx(b):
                sp.dma_start(ctxT[:, :, :], io["ctxT"].rearrange("(c p) n -> p c n", p=P)[:, :, bass.ds(b * S, S)]).then_inc(ctx_in, 16)

            def load_bias(b, par):
                sp.dma_start(nb[:, par, :, :], bias[bass.ds(b * S, S), :].rearrange("(t p) n -> p t n", p=P)).then_inc(nb_in, 16)
                sp.dma_start(nbT[:, par, :, :], biasT[bass.ds(b * S, S), :].rearrange("(t p) n -> p t n", p=P)).then_inc(nbT_in, 16)

            def store(parts, dram, ready, stored, count):
                sp.wait_ge(ready, count)
                sp.dma_start(dram.rearrange("r (c p) n -> p r c n", p=P), parts[:, :, :, :].bitcast(F32)).then_inc(stored, 16)

            def load_stack(g):
                h = slice(g * HG * DK, (g + 1) * HG * DK)
                for r in range(4):
                    for stack, dram, part in ((q_stack[g], q_parts, r % 2), (k_stack[g], k_parts, r // 2)):
                        sp.dma_start(stack[r * DK:(r + 1) * DK, :, :].bitcast(F32),
                                     dram[part, h, :].rearrange("(h d) n -> d h n", d=DK)).then_inc(stack_in[g], 16)
                sp.dma_start(q_stack[g][R4:R4 + 2, :, :].bitcast(F32), 
                             zrow[:, :].rearrange("p (a n) -> p a n", a=1).to_broadcast([2, HG, S])).then_inc(stack_in[g], 16)

            sp.wait_ge(set_up, SETUP)
            for w, name in ((wq, "wqT"), (wk, "wkT"), (wv, "wvT")):
                sp.dma_start(w[:, :, :], io[name].rearrange("(c p) n -> p c n", p=P)).then_inc(w_in, 16)
            load_ctx(0)
            load_bias(0, 0)
            sp.dma_start(wo[:, :, :], io["woT"].rearrange("(g p) n -> p g n", p=P)).then_inc(w_in, 16)
            for v, name in ((bq, "bq"), (bk, "bk")):
                sp.dma_start(v[:, :], io[name].rearrange("(c p) -> p c", p=P), allow_slow_non_contiguous=True).then_inc(w_in, 16)
            sp.dma_start(bv[:, :], io["bv"].rearrange("(a n) -> a n", a=1).to_broadcast([P, D])).then_inc(w_in, 16)
            store(kp, k_parts, misc_free, k_stored, FIRST.index("k1") + 1)
            store(qp, q_parts, qp_ready, q_stored, KC)
            sp.wait_ge(k_stored, 16)
            sp.wait_ge(q_stored, 16)
            for g in range(G):
                load_stack(g)
            sp.wait_ge(misc_full, FIRST.index("v1") + 1)
            load_ctx(1)
            with sp.Fori(0, B) as b:
                sp.wait_ge(exp_done, b * 32 + 2)
                for g in range(G):
                    sp.wait_ge(stack_in[g], b * LOAD + LOAD)
                store(kp, k_parts, misc_free, k_stored, b * nj + (nf + number("k1") + 1))
                load_bias(nxt(b), (b + 1) % 2)
                store(qp, q_parts, qp_ready, q_stored, b * KC + 2 * KC)
                for g in range(G):
                    sp.wait_ge(exp_done, b * 32 + (8 * g + 10))
                    if g == 0:
                        sp.wait_ge(k_stored, b * 16 + 32)
                        sp.wait_ge(q_stored, b * 16 + 32)
                    load_stack(g)
                    if g == 2:
                        load_ctx((b + 2) % B)
            for g in range(G):
                sp.wait_ge(stack_in[g], LOAD * (B + 1))
            sp.wait_ge(ctx_in, 16 * (B + 2))
            sp.wait_ge(nb_in, 16 * (B + 1))

        @block.tensor
        def _(pe):
            def bank_free(n):
                if not (isinstance(n, int) and n == 0):
                    pe.wait_ge(misc_free, n)

            def max_rows(n, a, par):
                bank_free(n)
                pe.wait_ge(max_done, a * SLOTS + SLOTS + 2)
                for t in range(TB):
                    last = pe.transpose(misc[0:HG, t * P:(t + 1) * P], negmax[:, par, t, :], ident[:, :])
                last.then_inc(misc_full, 1)

            def output(n, b, c):
                bank_free(n)
                pe.wait_ge(outT_ready, b * G + 1)
                for t in range(2):
                    for g in range(G):
                        tok = (2 * c + t) * P
                        last = pe.matmul(misc[:, t * D:(t + 1) * D], outT[:, g, tok:tok + P], wo[:, g, :],
                                         start=(g == 0), stop=(g == G - 1))
                last.then_inc(misc_full, 1)

            def prepare(n, name, b):
                bank_free(n)
                if name == "rv":
                    pe.wait_ge(nbT_in, b * 16 + 16)
                    for t in range(TB):
                        last = pe.matmul(misc[:, :], tiny16[:, :], nbT[:, b % 2, t, :], start=(t == 0), stop=(t == TB - 1))
                    last.then_inc(misc_full, 1)
                    return
                c = int(name[-1])
                if name[0] == "k":
                    pe.wait_ge(ctx_in, b * 16 + 16)
                    for i in range(KC):
                        last = pe.matmul(misc[:, :], wk[:, i, c * P:(c + 1) * P], ctxT[:, i, :], start=(i == 0), stop=(i == KC - 1))
                elif name[0] == "x":
                    pe.wait_ge(xn_ready, b * TB + TB)
                    for t in range(TB):
                        last = pe.transpose(misc[:, t * P:(t + 1) * P], xn[:, t, c * P:(c + 1) * P], ident[:, :])
                elif name[0] == "q":
                    for i in range(KC):
                        last = pe.matmul(misc[:, :], wq[:, i, c * P:(c + 1) * P], xT[:, i, :], start=(i == 0), stop=(i == KC - 1))
                else:
                    for t in range(2):
                        for i in range(KC):
                            tok = (2 * c + t) * P
                            last = pe.matmul(misc[:, t * D:(t + 1) * D], ctxT[:, i, tok:tok + P], wv[:, i, :],
                                             start=(i == 0), stop=(i == KC - 1))
                last.then_inc(misc_full, 1)

            def score_a(g, b, s, a, masked):
                h, t = s // TB, s % TB
                if s == 0:
                    pe.wait_ge(stack_in[g], b * LOAD + LOAD)
                    if masked:
                        pe.wait_ge(nb_in, b * 16 + 16)
                pe.wait_ge(max_done, a * SLOTS + s + 1)
                if masked:
                    pe.matmul(na[s % 2][:, :], ident16[:, :], nb[:, b % 2, t, :], start=True, stop=False)
                pe.matmul(na[s % 2][:, :], q_stack[g][:, h, t * P:(t + 1) * P], k_stack[g][:, h, :],
                          start=not masked, stop=True).then_inc(na_full, 1)

            def score_b(g, b, s, u, masked):
                t, h = s // HG, s % HG
                pair = s // 2
                if s == 0:
                    pe.wait_ge(m_in, u * 32 + 32)
                if s % 2 == 0:
                    pe.wait_ge(exp_done, u * (SLOTS // 2) + pair + 1)
                out = st[pair % 2][:, s % 2, :]
                if masked:
                    pe.matmul(out, ident16[:, :], nbT[:, b % 2, t, :], start=True, stop=False)
                last = pe.matmul(out, k_stack[g][:, h, t * P:(t + 1) * P], q_stack[g][:, h, :], start=not masked, stop=True)
                if s % 2:
                    last.then_inc(st_full, 1)

            def values(g, t):
                for h in range(HG):
                    last = pe.matmul(av[32 * h:32 * h + 32, :], vw[:, g, t, h, :], pr[:, t % 2, h, :],
                                     start=(t == 0), stop=(t == TB - 1), skip_group_check=True)
                last.then_inc(av_done, 1)

            def all_units(masked):
                for g in range(2):
                    for s in range(SLOTS):
                        score_a(g, 0, s, g, masked)
                    if g == 0:
                        max_rows(nf - 1, 0, 0)
                with pe.Fori(0, B) as b:
                    for g in range(G):
                        u = b * G + g
                        for s in range(SLOTS):
                            score_b(g, b, s, u, masked)
                            score_a((g + 2) % G, b if g < 2 else b + 1, s, u + 2, masked)
                            if s == 2:
                                pe.wait_ge(exp_done, u * (SLOTS // 2) + 2)
                                values((g - 1) % G, TB - 1)
                            elif s % 4 == 2:
                                t = s // 4 - 1
                                pe.wait_ge(exp_done, u * (SLOTS // 2) + 2 * t + 4)
                                if t == 0:
                                    pe.wait_ge(vw_ready, u + 1)
                                    pe.wait_ge(outT_ready, u + 1)
                                values(g, t)
                            for n, name in jobs_at(g, s):
                                job = b * nj + (nf + n)
                                if name == "m":
                                    max_rows(job, u + 1, (g + 1) % 2)
                                elif name[0] == "o":
                                    output(job, b, int(name[1]))
                                else:
                                    prepare(job, name, b + 1)

            pe.wait_ge(w_in, 16 * 7)
            for n, name in enumerate(FIRST[:-1]):
                if n == 0:
                    pe.wait_ge(set_up, SETUP)
                prepare(n, name, 0)
            for t in range(TB - 1):
                values(G - 1, t)
            flagged = pe.value_load(flag[0:1, 0:1], min_val=0, max_val=1)
            with pe.If(flagged > 0):
                all_units(True)
            with pe.Else():
                all_units(False)
            pe.wait_ge(exp_done, B * G * (SLOTS // 2) + 2)
            values(G - 1, TB - 1)
            for c in range(2):
                output(B * nj + nf + c, B, c)

        @block.scalar
        def _(act):
            def evacuate(n, name, b):
                c = int(name[-1])
                act.wait_ge(misc_full, n + 1)
                if name[0] == "k":
                    if not (isinstance(b, int) and b == 0):
                        act.wait_ge(k_stored, b * 16)
                    act.activation(kp[:, 0, c, :], misc[:, :], ACT.Identity, bias=bk[:, c:c + 1]).then_inc(k_head, 1)
                else:
                    act.copy(xT[:, c, :], misc[:, :]).then_inc(misc_free, 1)

            def send_rows(g, n):
                act.wait_ge(misc_free, n + 1)
                for r in range(2):
                    act.dma_start(q_stack[g][R4 + r:R4 + r + 1, :, :].bitcast(F32), mrow[:, r, :].bitcast(F32)).then_inc(m_in, 16)

            act.wait_ge(w_in, 16 * 7)
            act.wait_ge(set_up, SETUP)
            for n, name in enumerate(FIRST):
                if name[0] in "kx":
                    evacuate(n, name, 0)
            send_rows(0, FIRST.index("m"))
            with act.Fori(0, B) as b:
                for g in range(G):
                    u = b * G + g
                    for s in range(SLOTS):
                        if s == 4:
                            send_rows((g + 1) % G, b * nj + (nf + [n for n, j in enumerate(JOBS) if j[0] == "m"][g]))
                        if s % 2:
                            pair = s // 2
                            act.wait_ge(st_full, u * (SLOTS // 2) + pair + 1)
                            if pair % 2 == 0:
                                act.wait_ge(av_done, u * TB + pair // 2 + 3)
                            h = 2 * (pair % 2)
                            act.activation(pr[:, pair // 2 % 2, h:h + 2, :], st[pair % 2][:, :, :], ACT.Exp,
                                           scale=DK ** -0.5).then_inc(exp_done, 1)
                        for n, name in jobs_at(g, s):
                            if name[0] in "kx":
                                evacuate(b * nj + (nf + n), name, b + 1)
            act.wait_ge(m_in, 32 * (B * G + 1))

        @block.gpsimd
        def _(pool):
            def split_q(c, n, b):
                pool.wait_ge(misc_free, n + 1)
                if not (isinstance(b, int) and b == 0):
                    pool.wait_ge(q_stored, b * 16)
                pool.tensor_tensor(qp[:, 0, c, :].rearrange("p (t n) -> p t n", n=P), qf[:, c, :].rearrange("p (t n) -> p t n", n=P),
                                   ones[:, :].rearrange("p (a n) -> p a n", a=1).to_broadcast([P, TB, P]), ALU.mult).then_inc(q_head, 1)
                pool.wait_ge(q_head, b * KC + c + 1)
                pool.tensor_tensor(qp[:, 1, c, :], qf[:, c, :], qp[:, 0, c, :].bitcast(F32), ALU.subtract).then_inc(qp_ready, 1)

            def move_values(g, u, n):
                if n is not None:
                    pool.wait_ge(misc_free, n + 1)
                if not isinstance(u, int):
                    pool.wait_ge(av_done, (u - (G - 1)) * TB + 4)
                for t in range(TB):
                    v = vstage[:, t, g * HG * DK:(g + 1) * HG * DK].rearrange("p (h d) -> p h d", d=DK)
                    last = pool.tensor_tensor(vw[:, g, t, :, 0:DK], v, ones[:, 0:HG * DK].rearrange("p (h d) -> p h d", d=DK), ALU.mult)
                last.then_inc(vw_ready, 1)

            pool.memset(pr[:, :, :, :], 1.0).then_inc(set_up, 1)
            pool.memset(vw[:, :, :, :, 0:DK], 0.0).then_inc(set_up, 1)
            pool.memset(vw[:, :, :, :, DK:32], 1.0).then_inc(set_up, 1)
            pool.memset(outT[:, :, :], 0.0).then_inc(set_up, 1)
            pool.memset(tiny16[:, :], -1.0 / MASKED).then_inc(set_up, 1)
            for c in range(KC):
                split_q(c, FIRST.index(f"q{c}"), 0)
            for g in range(G - 1):
                move_values(g, g, FIRST.index("v1"))
            with pool.Fori(0, B) as b:
                for g in range(G):
                    u = b * G + g
                    if g == 0:
                        move_values(G - 1, u + G - 1, None)
                    if g == 0:
                        for c in range(KC):
                            split_q(c, b * nj + (nf + number(f"q{c}")), b + 1)
                    else:
                        move_values(g - 1, u + G - 1, b * nj + (nf + number("v1")))

        @block.vector
        def _(dve):
            def normalise(b, mean_b):
                for i in range(TB):
                    t = mean_b * TB + i
                    dve.tensor_scalar(xn[:, i, :], x[:, bass.ds(t, 1), :], mv[:, bass.ds(t, 1), 0],
                                      rstd[:, bass.ds(t, 1)], ALU.subtract, ALU.mult).then_inc(xn_ready, 1)

            def maximum(g, s, a):
                dve.wait_ge(na_full, a * SLOTS + s + 1)
                dve.tensor_reduce(negmax[:, g % 2, s % TB, s // TB:s // TB + 1], na[s % 2][:, :], AX.X, ALU.max,
                                  negate=True).then_inc(max_done, 1)

            def evacuate(n, name, b, a, bx):
                dve.wait_ge(misc_full, n + 1)
                c = int(name[-1]) if name[-1].isdigit() else 0
                if name == "m":
                    if not (isinstance(a, int) and a == 0):
                        dve.wait_ge(m_in, a * 32)
                    dve.tensor_copy(mrow[:, 0, :], misc[0:HG, :]).then_inc(mh_ready, 1)
                    dve.wait_ge(mh_ready, a + 1)
                    dve.tensor_tensor(mrow[:, 1, :], misc[0:HG, :], mrow[:, 0, :].bitcast(F32), ALU.subtract).then_inc(misc_free, 1)
                elif name[0] == "k":
                    dve.wait_ge(k_head, b * KC + c + 1)
                    dve.scalar_tensor_tensor(out=kp[:, 1, c, :], in0=misc[:, :], scalar=bk[:, c:c + 1],
                                             in1=kp[:, 0, c, :].bitcast(F32), op0=ALU.add, op1=ALU.subtract).then_inc(misc_free, 1)
                elif name == "rv":
                    dve.tensor_scalar(rv[:, :], misc[:, :], 0.5 - S, None, ALU.is_gt).then_inc(misc_free, 1)
                elif name[0] == "q":
                    if not (isinstance(b, int) and b == 0):
                        dve.wait_ge(qp_ready, b * KC)
                    dve.scalar_tensor_tensor(out=qf[:, c, :], in0=misc[:, :], scalar=bq[:, c:c + 1], in1=rv[:, :],
                                             op0=ALU.add, op1=ALU.mult).then_inc(misc_free, 1)
                elif name[0] == "v":
                    if not (isinstance(b, int) and b == 0):
                        dve.wait_ge(vw_ready, b * G)
                    dve.tensor_tensor(vstage[:, 2 * c:2 * c + 2, :], misc[:, :].rearrange("p (t n) -> p t n", t=2),
                                      bv[:, :].rearrange("p (a n) -> p a n", a=1).to_broadcast([P, 2, D]), ALU.add).then_inc(misc_free, 1)
                else:
                    t = bx * TB + 2 * c
                    dve.tensor_tensor(x[:, bass.ds(t, 2), :], misc[:, :].rearrange("p (t n) -> p t n", t=2),
                                      x[:, bass.ds(t, 2), :], ALU.add).then_inc(misc_free, 1)

            def divide(g, u):
                dve.wait_ge(av_done, u * TB + TB)
                dve.memset(tick[:, :], 0.0)
                dve.stream_shuffle(sums[:, :], av[:, :], [DK + i % DK for i in range(32)]).then_inc(sums_ready, 1)
                dve.wait_ge(sums_ready, u + 1)
                dve.reciprocal(rec[:, :], sums[:, :]).then_inc(rec_ready, 1)
                dve.wait_ge(rec_ready, u + 1)
                dve.tensor_tensor(outT[:, g, :], av[:, :], rec[:, :], ALU.mult).then_inc(outT_ready, 1)

            dve.tensor_copy(ident16[:, :], ident[:, :]).then_inc(set_up, 1)
            for g in range(G):
                dve.memset(k_stack[g][R4:P, :, :].bitcast(F32), 1.0).then_inc(set_up, 1)
                dve.memset(q_stack[g][R4:P, :, :].bitcast(F32), 0.0).then_inc(set_up, 1)
            dve.memset(zrow[:, :], 0.0).then_inc(set_up, 1)
            for i in range(2):
                dve.memset(rec[:, i:i + 1], 0.0).then_inc(max_done, 1)
                dve.memset(sums[:, i:i + 1], 0.0).then_inc(exp_done, 1)
            dve.wait_ge(max_done, 2)
            dve.wait_ge(exp_done, 2)
            dve.wait_ge(w_in, 16 * 7)
            normalise(0, 0)
            for n, name in enumerate(FIRST[:-1]):
                if name[0] != "x":
                    evacuate(n, name, 0, None, None)
            for g in range(2):
                for s in range(SLOTS):
                    maximum(g, s, g)
                if g == 0:
                    evacuate(nf - 1, "m", None, 0, None)
            with dve.Fori(0, B) as b:
                for g in range(G):
                    u = b * G + g
                    for s in range(SLOTS):
                        maximum(g + 2, s, u + 2)
                        if s == 3:
                            divide((g - 1) % G, u)
                        if (g, s) == (0, 4):
                            normalise(b + 1, (b + 1) % B)
                        for n, name in jobs_at(g, s):
                            if name[0] != "x":
                                evacuate(b * nj + (nf + n), name, b + 1, u + 1, (b + (B - 1)) % B)
            divide(G - 1, B * G)
            for c in range(2):
                evacuate(B * nj + nf + c, f"o{c}", None, None, B - 1)
            dve.wait_ge(misc_free, B * nj + nf + 2)


def self_gates(nc, ws_in, x, mv, rstd, ident, iota8, xT_d, gT_d):
    with ExitStack() as ctx:
        m = Names(nc, ctx, "sg")
        xn = m.sb("xn", [P, 4, D])
        xt = m.sb("xt", [P, KC, B * S])
        ws = m.sb("ws", [P, KC, SH])
        sig, top, topf = m.sb("sig", [P, NT, SH]), m.sb("top", [P, NT, 8]), m.sb("topf", [P, NT, 8])
        topi = m.sb("topi", [P, NT, 8], U32)
        hot = m.sb("hot", [P, STOP, NT, SH])
        kept = m.sb("kept", [P, 2, NT, SH])
        gate = m.sb("gate", [P, NT, SH])
        gT = m.sb("gT", [SH, B * S])
        xtp = [m.ps(f"xtp{i}", [P, KC, P]) for i in range(2)]
        lg = m.ps("lg", [P, NT, SH])
        gtp = [m.ps(f"gtp{i}", [SH, S]) for i in range(2)]
        ws_in_s, xn_ready, xtp_ready, xt_ready, lg_ready, sig_ready, step = (
            m.sem(n) for n in ("ws_in", "xn_ready", "xtp_ready", "xt_ready", "lg_ready", "sig_ready", "step"))
        gate_ready, gtp_ready, gT_ready, stored = (m.sem(n) for n in ("gate_ready", "gtp_ready", "gT_ready", "stored"))
        block = ctx.enter_context(nc.Block())

        @block.sync
        def _(sp):
            sp.dma_start(ws[:, :, :], ws_in.rearrange("(c p) e -> p c e", p=P)).then_inc(ws_in_s, 16)
            for b in range(B):
                sp.wait_ge(xt_ready, (b + 1) * TB)
                sp.dma_start(xT_d.rearrange("(c p) n -> p c n", p=P)[:, :, b * S:(b + 1) * S], xt[:, :, b * S:(b + 1) * S]).then_inc(stored, 16)
            sp.wait_ge(gT_ready, B)
            sp.dma_start(gT_d, gT[:, :]).then_inc(stored, 16)
            sp.wait_ge(stored, 16 * (B + 1))

        @block.tensor
        def _(pe):
            def gate_tile(t):
                pe.wait_ge(xt_ready, t + 1)
                for c in range(KC):
                    last = pe.matmul(lg[:, t, :], xt[:, c, t * P:(t + 1) * P], ws[:, c, :], start=(c == 0), stop=(c == KC - 1))
                last.then_inc(lg_ready, 1)

            pe.wait_ge(ws_in_s, 16)
            for t in range(NT):
                pe.wait_ge(xn_ready, t + 1)
                if t >= 2:
                    pe.wait_ge(xt_ready, t - 1)
                for c in range(KC):
                    last = pe.transpose(xtp[t % 2][:, c, :], xn[:, t % 4, c * P:(c + 1) * P], ident[:, :])
                last.then_inc(xtp_ready, 1)
                if t >= 1:
                    gate_tile(t - 1)
            gate_tile(NT - 1)
            pe.wait_ge(gate_ready, 1)
            for b in range(B):
                if b >= 2:
                    pe.wait_ge(gT_ready, b - 1)
                for t in range(TB):
                    last = pe.transpose(gtp[b % 2][:, t * P:(t + 1) * P], gate[:, b * TB + t, :], ident[:, :])
                last.then_inc(gtp_ready, 1)

        @block.scalar
        def _(act):
            for t in range(NT):
                act.wait_ge(xtp_ready, t + 1)
                act.copy(xt[:, :, t * P:(t + 1) * P], xtp[t % 2][:, :, :]).then_inc(xt_ready, 1)
            act.wait_ge(lg_ready, NT)
            act.activation(sig[:, :, :], lg[:, :, :], ACT.Sigmoid).then_inc(sig_ready, 1)
            for b in range(B):
                act.wait_ge(gtp_ready, b + 1)
                act.copy(gT[:, b * S:(b + 1) * S], gtp[b % 2][:, :]).then_inc(gT_ready, 1)

        @block.vector
        def _(dve):
            n = [0]

            def then(ins):
                n[0] += 1
                ins.then_inc(step, 1)
                dve.wait_ge(step, n[0])

            for t in range(NT):
                if t >= 4:
                    dve.wait_ge(xtp_ready, t - 3)
                dve.tensor_scalar(xn[:, t % 4, :], x[:, t, :], mv[:, t, 0:1], rstd[:, t:t + 1],
                                  ALU.subtract, ALU.mult).then_inc(xn_ready, 1)
            dve.wait_ge(sig_ready, 1)
            for t in range(NT):
                last = dve.max(top[:, t, :], sig[:, t, :])
            then(last)
            for t in range(NT):
                last = dve.max_index(topi[:, t, :], top[:, t, :], sig[:, t, :])
            then(last)
            then(dve.tensor_copy(topf[:, :, :], topi[:, :, :]))
            heads = iota8[:, :].rearrange("p (a e) -> p a e", a=1).to_broadcast([P, NT, SH])
            for j in range(STOP):
                ins = dve.tensor_tensor(hot[:, j, :, :], topf[:, :, j:j + 1].to_broadcast([P, NT, SH]), heads, ALU.is_equal)
            then(ins)
            then(dve.tensor_tensor(kept[:, 0, :, :], hot[:, 0, :, :], hot[:, 1, :, :], ALU.add))
            then(dve.tensor_tensor(kept[:, 1, :, :], kept[:, 0, :, :], hot[:, 2, :, :], ALU.add))
            dve.tensor_tensor(gate[:, :, :], sig[:, :, :], kept[:, 1, :, :], ALU.mult).then_inc(gate_ready, 1)


def self_attention(nc, io, x, ident, ones, xT_d, gT_d):
    with ExitStack() as ctx:
        m = Names(nc, ctx, "sa")
        C = SH // 2
        H = SDK
        wq, wk, wv = (m.sb(n, [P, KC, C * P]) for n in ("wq", "wk", "wv"))
        wo, bo = m.sb("wo", [P, C, D]), m.sb("bo", [SH, D])
        sel = m.sb("sel", [SH, SH * H])
        xT, gT = m.sb("xT", [P, KC, S]), m.sb("gT", [SH, S])
        part = {n: m.sb(n, [P, S], F32R) for n in ("qh", "ql", "kh", "kl")}
        q1, q2, k1, k2 = ([m.sb(f"{n}_{c}", [P, 2, S], F32R) for c in range(C)] for n in ("q1", "q2", "k1", "k2"))
        zrow = m.sb("zrow", [2, S])
        vw = m.sb("vw", [P, C, TB, P])
        negmax = m.sb("negmax", [P, 2, 2, TB])
        parts = m.sb("parts", [P, 2, 2, TB, 2])
        pr = m.sb("pr", [P, TB, 2, S])
        acc = m.sb("acc", [P, 2, S])
        rec, factor = m.sb("rec", [P, S]), m.sb("factor", [P, S])
        outT = m.sb("outT", [P, C, S])
        na = [m.ps(f"na{i}", [P, S]) for i in range(2)]
        st = [m.ps(f"st{i}", [P, 2, S]) for i in range(2)]
        av, misc = m.ps("av", [P, S]), m.ps("misc", [P, S])

        w_in, set_up, sel_set = m.sem("w_in"), m.sem("set_up"), m.sem("sel_set")
        xT_in, gT_in = m.sem("xT_in"), m.sem("gT_in")
        head_ready = m.sem("head_ready")
        stack_in = [m.sem(f"stack_in{c}") for c in range(C)]
        na_full, max_done, st_full, exp_done = m.sem("na_full"), m.sem("max_done"), m.sem("st_full"), m.sem("exp_done")
        mh_ready, ml_ready = m.sem("mh_ready"), m.sem("ml_ready")
        av_done, acc_done, outT_ready = m.sem("av_done"), m.sem("acc_done"), m.sem("outT_ready")
        misc_full, misc_free = m.sem("misc_full"), m.sem("misc_free")
        block = ctx.enter_context(nc.Block())

        SETUP = 5 + 3 * C
        WEIGHTS = 16 * 5
        SLOTS = 2 * TB
        LOAD = 16 * 13
        JOBS = []
        for g in range(C):
            JOBS += [("m0", g, 0), ("m1", g, 1), ("sum", g, 2), ("gate", g, 3), ("q", g, 4), ("k", g, 5), ("v", g, 6)]
            if g == 0:
                JOBS += [("o0", g, 6), ("o1", g, 7)]
        FIRST = ["q", "k", "v"] * 3 + ["m0", "m1"]
        LAST = ["sum", "gate", "o0", "o1"]
        nj, nf = len(JOBS), len(FIRST)

        def job(b, g, name):
            return b * nj + (nf + next(n for n, j in enumerate(JOBS) if j[0] == name and j[1] == g))

        def jobs_at(g, s):
            return [j[0] for j in JOBS if j[1:] == (g, s)]

        def last_job(name):
            return B * nj + nf + LAST.index(name)

        @block.sync
        def _(sp):
            def load_x(n):
                sp.dma_start(xT[:, :, :], xT_d.rearrange("(c p) n -> p c n", p=P)[:, :, bass.ds(n, S)]).then_inc(xT_in, 16)

            def stack(c, pairs):
                for dst, lo, name in pairs:
                    for h in range(2):
                        sp.dma_start(dst[c][lo:lo + H, h, :].bitcast(F32), part[name][h * H:(h + 1) * H, :].bitcast(F32)).then_inc(stack_in[c], 16)

            def load_stacks(c, nq):
                sp.wait_ge(misc_free, nq + 1)
                stack(c, ((q1, 0, "qh"), (q1, H, "ql"), (q2, 0, "qh")))
                sp.dma_start(q2[c][H:H + 2, :, :].bitcast(F32), zrow[:, :].rearrange("p (a n) -> p a n", a=1).to_broadcast([2, 2, S])).then_inc(stack_in[c], 16)
                sp.wait_ge(misc_free, nq + 2)
                stack(c, ((k1, 0, "kh"), (k1, H, "kh"), (k2, 0, "kl")))

            for w, name in ((wq, "sWq"), (wk, "sWk"), (wv, "sWv"), (wo, "sWo")):
                sp.dma_start(w[:, :, :], io[name].rearrange("(c p) n -> p c n", p=P)).then_inc(w_in, 16)
            sp.dma_start(bo[:, :], io["sbo"]).then_inc(w_in, 16)
            load_x(0)
            sp.wait_ge(set_up, SETUP)
            for c in range(3):
                load_stacks(c, 3 * c)
            with sp.Fori(0, B) as b:
                for g in range(C):
                    u = b * C + g
                    load_stacks((g + 3) % C, job(b, g, "q"))
                    if g == 0:
                        after = sp.snap(((b + 1) % B) * S)
                        sp.wait_ge(misc_full, job(b, g, "v") + 1)
                        load_x(after)
                        sp.wait_ge(misc_full, job(b, g, "o1") + 1)
                        sp.dma_start(gT[:, :], gT_d[:, bass.ds(b * S, S)]).then_inc(gT_in, 16)
            for c in range(C):
                sp.wait_ge(stack_in[c], LOAD * (B + 1 if c < 3 else B))
            sp.wait_ge(xT_in, 16 * (B + 1))
            sp.wait_ge(gT_in, 16 * B)

        @block.tensor
        def _(pe):
            def bank_free(n):
                if not (isinstance(n, int) and n == 0):
                    pe.wait_ge(misc_free, n)

            def max_rows(n, a, par, h):
                bank_free(n)
                pe.wait_ge(ml_ready, a * 2 + (h + 1))
                for t in range(TB):
                    last = pe.matmul(misc[H:H + 2, t * P:(t + 1) * P], parts[:, par, h, t, :], ident[:, :], start=True, stop=True)
                last.then_inc(misc_full, 1)

            def project(n, name, c, b):
                bank_free(n)
                if name == "q":
                    pe.wait_ge(xT_in, b * 16 + 16)
                if name == "v":
                    for t in range(TB):
                        for i in range(KC):
                            last = pe.matmul(misc[:, t * P:(t + 1) * P], xT[:, i, t * P:(t + 1) * P], wv[:, i, c * P:(c + 1) * P],
                                             start=(i == 0), stop=(i == KC - 1))
                else:
                    w = wq if name == "q" else wk
                    for i in range(KC):
                        last = pe.matmul(misc[:, :], w[:, i, c * P:(c + 1) * P], xT[:, i, :], start=(i == 0), stop=(i == KC - 1))
                last.then_inc(misc_full, 1)

            def sums(n, u):
                bank_free(n)
                pe.wait_ge(acc_done, u * 3 + 3)
                for h in range(2):
                    last = pe.matmul(misc[h * H:(h + 1) * H, :], ones[:, 0:H], acc[:, h, :], start=True, stop=True, skip_group_check=True)
                last.then_inc(misc_full, 1)

            def gates(n, c):
                bank_free(n)
                pe.matmul(misc[:, :], sel[:, c * P:(c + 1) * P], gT[:, :], start=True, stop=True).then_inc(misc_full, 1)

            def output(n, b, i):
                bank_free(n)
                pe.wait_ge(outT_ready, b * C + 1)
                for t in range(2):
                    tok = (2 * i + t) * P
                    out = misc[:, t * D:(t + 1) * D]
                    for c in range(C):
                        pe.matmul(out, outT[:, c, tok:tok + P], wo[:, c, :], start=(c == 0), stop=False)
                    last = pe.matmul(out, gT[:, tok:tok + P], bo[:, :], start=False, stop=True)
                last.then_inc(misc_full, 1)

            def score_a(c, b, s, a):
                h, t = s // TB, s % TB
                if s == 0:
                    pe.wait_ge(stack_in[c], b * LOAD + LOAD)
                pe.wait_ge(max_done, a * SLOTS + (s + 1))
                pe.matmul(na[s % 2][:, :], q1[c][:, h, t * P:(t + 1) * P], k1[c][:, h, :], start=True, stop=False)
                pe.matmul(na[s % 2][:, :], q2[c][:, h, t * P:(t + 1) * P], k2[c][:, h, :], start=False, stop=True).then_inc(na_full, 1)

            def score_b(c, s, u):
                t, h = s // 2, s % 2
                if h == 0:
                    pe.wait_ge(exp_done, u * TB + (t + 1))
                out = st[t % 2][:, h, :]
                pe.matmul(out, k1[c][:, h, t * P:(t + 1) * P], q1[c][:, h, :], start=True, stop=False)
                last = pe.matmul(out, k2[c][:, h, t * P:(t + 1) * P], q2[c][:, h, :], start=False, stop=True)
                if h:
                    last.then_inc(st_full, 1)

            def values(c, t):
                for h in range(2):
                    last = pe.matmul(av[h * H:(h + 1) * H, :], vw[:, c, t, h * H:(h + 1) * H], pr[:, t, h, :],
                                     start=(t == 0), stop=(t == TB - 1), skip_group_check=True)
                last.then_inc(av_done, 1)

            pe.wait_ge(w_in, WEIGHTS)
            pe.wait_ge(set_up, SETUP)
            pe.wait_ge(sel_set, 3)
            for n, name in enumerate(FIRST[:-2]):
                project(n, name, n // 3, 0)
            for t in range(TB - 1):
                values(C - 1, t)
            for a in range(2):
                for s in range(SLOTS):
                    score_a(a, 0, s, a)
                if a == 0:
                    for h in range(2):
                        max_rows(nf - 2 + h, 0, 0, h)
            with pe.Fori(0, B) as b:
                for g in range(C):
                    u = b * C + g
                    for s in range(SLOTS):
                        if s == 0:
                            pe.wait_ge(misc_free, b * nj + (nf if g == 0 else nf + next(n for n, j in enumerate(JOBS) if j == ("m1", g - 1, 1)) + 1))
                        score_b(g, s, u)
                        score_a((g + 2) % C, b if g < 2 else b + 1, s, u + 2)
                        if s == 1:
                            pe.wait_ge(exp_done, u * TB + 2)
                            values((g - 1) % C, TB - 1)
                        if s >= 5:
                            t = s - 5
                            pe.wait_ge(exp_done, u * TB + (t + 3))
                            if t == 0:
                                pe.wait_ge(outT_ready, u + 1)
                            values(g, t)
                        for name in jobs_at(g, s):
                            n = job(b, g, name)
                            if name[0] == "m":
                                max_rows(n, u + 1, (g + 1) % 2, int(name[1]))
                            elif name == "sum":
                                sums(n, u)
                            elif name == "gate":
                                if g == 1:
                                    pe.wait_ge(gT_in, b * 16 + 16)
                                gates(n, (g - 1) % C)
                            elif name[0] == "o":
                                output(n, b, int(name[1]))
                            else:
                                project(n, name, (g + 3) % C, b if g == 0 else b + 1)
            pe.wait_ge(exp_done, B * C * TB + 2)
            values(C - 1, TB - 1)
            sums(last_job("sum"), B * C)
            gates(last_job("gate"), C - 1)
            for i in range(2):
                output(last_job(f"o{i}"), B, i)

        @block.scalar
        def _(act):
            def head(n, name, k, prev):
                act.wait_ge(misc_full, n + 1)
                if prev is not None:
                    act.wait_ge(*prev)
                act.copy(part[name + "h"][:, :], misc[:, :]).then_inc(head_ready, 1)

            def v_out(n, c):
                act.wait_ge(misc_full, n + 1)
                act.copy(vw[:, c, :, :], misc[:, :].rearrange("p (t n) -> p t n", n=P)).then_inc(misc_free, 1)

            def m_out(n, c, h):
                act.wait_ge(misc_full, n + 1)
                act.copy(q2[c][H:H + 2, h, :], misc[H:H + 2, :]).then_inc(misc_free, 1)

            act.wait_ge(set_up, SETUP)
            for n, name in enumerate(FIRST[:-2]):
                c = n // 3
                if name == "v":
                    v_out(n, c)
                else:
                    head(n, name, None, (stack_in[c - 1], LOAD) if c else None)
            for h in range(2):
                m_out(nf - 2 + h, 0, h)
            with act.Fori(0, B) as b:
                for g in range(C):
                    u = b * C + g
                    for s in range(SLOTS):
                        if s % 2:
                            t = s // 2
                            act.wait_ge(st_full, u * TB + (t + 1))
                            act.wait_ge(av_done, u * TB + (t + 1))
                            act.wait_ge(acc_done, u * 3 + max(t, 1))
                            act.activation(pr[:, t, :, :], st[t % 2][:, :, :], ACT.Exp, scale=H ** -0.5).then_inc(exp_done, 1)
                        for name in jobs_at(g, s):
                            n = job(b, g, name)
                            if name in "qk":
                                head(n, name, None, (stack_in[(g + 2) % C], b * LOAD + (2 * LOAD if g >= 2 else LOAD)))
                            elif name == "v":
                                v_out(n, (g + 3) % C)
                            elif name[0] == "m":
                                m_out(n, (g + 1) % C, int(name[1]))

        @block.gpsimd
        def _(pool):
            pool.memset(pr[:, :, :, :], 1.0).then_inc(set_up, 1)
            pool.memset(vw[:, :, :, :], 0.0).then_inc(set_up, 1)
            pool.memset(outT[:, :, :], 0.0).then_inc(set_up, 1)
            pool.memset(gT[:, :], 0.0).then_inc(set_up, 1)
            for i in range(3):
                pool.memset(acc[:, :, i * P:(i + 1) * P] if i < 2 else acc[:, :, 2 * P:S], 1.0).then_inc(acc_done, 1)
            pool.memset(sel[:, :], 1.0).then_inc(sel_set, 1)
            pool.wait_ge(sel_set, 1)
            pool.affine_select(out=sel[:, :], in_=sel[:, :], compare_op=ALU.is_ge, fill=0.0,
                               base=0, pattern=[[1, SH * H]], channel_multiplier=-H).then_inc(sel_set, 1)
            pool.wait_ge(sel_set, 2)
            pool.affine_select(out=sel[:, :], in_=sel[:, :], compare_op=ALU.is_ge, fill=0.0,
                               base=H - 1, pattern=[[-1, SH * H]], channel_multiplier=H).then_inc(sel_set, 1)
            with pool.Fori(0, B) as b:
                for g in range(C):
                    u = b * C + g
                    pool.wait_ge(misc_full, job(b, g, "sum") + 1)
                    pool.wait_ge(exp_done, u * TB + 4)
                    pool.tensor_tensor(acc[:, :, :], pr[:, 0, :, :], pr[:, 1, :, :], ALU.add).then_inc(acc_done, 1)
                    for t in (2, 3):
                        pool.wait_ge(exp_done, u * TB + (t + 3))
                        pool.wait_ge(acc_done, u * 3 + (t + 2))
                        pool.tensor_tensor(acc[:, :, :], acc[:, :, :], pr[:, t, :, :], ALU.add).then_inc(acc_done, 1)

        @block.vector
        def _(dve):
            def maximum(par, s, a):
                dve.wait_ge(na_full, a * SLOTS + (s + 1))
                h, t = s // TB, s % TB
                dve.tensor_reduce(negmax[:, par, h, t:t + 1], na[s % 2][:, :], AX.X, ALU.max, negate=True).then_inc(max_done, 1)
                if t == TB - 1:
                    dve.wait_ge(max_done, a * SLOTS + (s + 3))
                    dve.tensor_copy(parts[:, par, h, :, 0].bitcast(F32R), negmax[:, par, h, :]).then_inc(mh_ready, 1)
                    dve.wait_ge(mh_ready, a * 2 + (h + 1))
                    dve.tensor_tensor(parts[:, par, h, :, 1].bitcast(F32R), negmax[:, par, h, :], parts[:, par, h, :, 0], ALU.subtract).then_inc(ml_ready, 1)

            def rest(n, name, k):
                dve.wait_ge(head_ready, k + 1)
                dve.tensor_tensor(part[name + "l"][:, :], misc[:, :], part[name + "h"][:, :].bitcast(F32), ALU.subtract).then_inc(misc_free, 1)

            def reciprocal(n):
                dve.wait_ge(misc_full, n + 1)
                dve.reciprocal(rec[:, :], misc[:, :]).then_inc(misc_free, 1)

            def divide(n, c, u):
                dve.wait_ge(misc_full, n + 1)
                dve.tensor_tensor(factor[:, :], misc[:, :], rec[:, :], ALU.mult).then_inc(misc_free, 1)
                dve.wait_ge(av_done, u * TB + 4)
                dve.wait_ge(misc_free, n + 1)
                dve.tensor_tensor(outT[:, c, :], av[:, :], factor[:, :], ALU.mult).then_inc(outT_ready, 1)

            def add(n, i, b):
                dve.wait_ge(misc_full, n + 1)
                t = b * TB + 2 * i
                tiles = x[:, t:t + 2, :] if isinstance(b, int) else x[:, bass.ds(t, 2), :]
                dve.tensor_tensor(tiles, misc[:, :].rearrange("p (t n) -> p t n", t=2), tiles, ALU.add).then_inc(misc_free, 1)

            for c in range(C):
                dve.memset(k2[c][H:P, :, :].bitcast(F32), 1.0).then_inc(set_up, 1)
                dve.memset(q2[c][H:P, :, :].bitcast(F32), 0.0).then_inc(set_up, 1)
                dve.memset(q1[c][H:P, 0, 0:1].bitcast(F32), 0.0).then_inc(set_up, 1)
            dve.memset(zrow[:, :], 0.0).then_inc(set_up, 1)
            for i in range(2):
                dve.memset(rec[:, i:i + 1], 0.0).then_inc(max_done, 1)
                dve.memset(factor[:, i:i + 1], 0.0).then_inc(exp_done, 1)
            dve.wait_ge(max_done, 2)
            dve.wait_ge(exp_done, 2)
            k = 0
            for n, name in enumerate(FIRST[:-2]):
                if name != "v":
                    rest(n, name, k)
                    k += 1
            for a in range(2):
                for s in range(SLOTS):
                    maximum(a, s, a)
            with dve.Fori(0, B) as b:
                for g in range(C):
                    u = b * C + g
                    for s in range(SLOTS):
                        maximum(g % 2, s, u + 2)
                        for name in jobs_at(g, s):
                            n = job(b, g, name)
                            if name in "qk":
                                rest(n, name, u * 2 + (6 + "qk".index(name)))
                            elif name == "sum":
                                reciprocal(n)
                            elif name == "gate":
                                divide(n, (g - 1) % C, u)
                            elif name[0] == "o":
                                add(n, int(name[1]), (b + (B - 1)) % B)
            reciprocal(last_job("sum"))
            divide(last_job("gate"), C - 1, B * C)
            for i in range(2):
                add(last_job(f"o{i}"), i, B - 1)
            dve.wait_ge(misc_free, last_job("o1") + 1)


def build(nc, io):
    with ExitStack() as ctx:
        m = Names(nc, ctx, "all")
        ident, before, ones = m.sb("ident", [P, P]), m.sb("before", [P, P]), m.sb("ones", [P, P])
        iota8 = m.sb("iota8", [P, E])
        x = m.sb("x", [P, NT, D])
        stats = m.sb("stats", [P, NT, 6])
        mv, rstd = m.sb("mv", [P, NT, 2]), m.sb("rstd", [P, NT])
        weight = m.sb("weight", [P, TOPK, NT])
        place = m.sb("place", [P, TOPK, NT], U32)
        tile_at = m.sb("tile_at", [P, E + 1], I32)
        flag = m.sb("flag", [P, 1], I32)
        rows = nc.dram_tensor("expert_rows", ((MAXT + 1) * P, D), F32).ap()
        outs = nc.dram_tensor("expert_outs", (MAXT * P, D), F32).ap()
        bias = nc.dram_tensor("mask_bias", (B * S, S), BF16).ap()
        biasT = nc.dram_tensor("mask_bias_T", (B * S, S), BF16).ap()
        q_parts = nc.dram_tensor("q_parts", (2, D, S), F32).ap()
        k_parts = nc.dram_tensor("k_parts", (2, D, S), F32).ap()
        xT_d = nc.dram_tensor("normed_T", (D, B * S), F32).ap()
        gT_d = nc.dram_tensor("gates_T", (SH, B * S), F32).ap()

        constants(nc, ident, before, ones, iota8)
        feature_attention(nc, io["x"], io["ctxT"], x, stats, ident)
        with ExitStack() as c2:
            xn = Names(nc, c2, "all").sb("xn", [P, NT, D])
            route(nc, io["gateT"], rows, outs, x, stats, ident, before, ones, iota8, xn, weight, place, tile_at)
        experts(nc, io["gateupT"], io["downT"], rows, outs, ident, tile_at)
        combine(nc, outs, x, weight, place)
        masks(nc, io["mask"], io["maskT"], bias, biasT, flag, ones)
        norm_stats(nc, x, mv, rstd, "ns1")
        cross_attention(nc, io, x, mv, rstd, ident, ones, bias, biasT, flag, q_parts, k_parts)
        norm_stats(nc, x, mv, rstd, "ns2")
        self_gates(nc, io["sWs"], x, mv, rstd, ident, iota8, xT_d, gT_d)
        self_attention(nc, io, x, ident, ones, xT_d, gT_d)

        out_done = m.sem("out_done")
        with nc.Block() as block:
            @block.sync
            def _(sp):
                sp.dma_start(io["out"].rearrange("(t p) d -> p t d", p=P), x[:, :, :]).then_inc(out_done, 16)
                sp.wait_ge(out_done, 16)


def cross_output_rows(wo, bo):
    import numpy as np
    rows = np.zeros((HEADS, 32, D), np.float32)
    rows[:, :DK, :] = np.asarray(wo).T.reshape(HEADS, DK, D)
    rows[0, DK, :] = np.asarray(bo)
    return rows.reshape(HEADS * 32, D)


def layout(a):
    import numpy as np
    f = lambda v: np.ascontiguousarray(v)
    return {
        "x": f(np.reshape(a["x"], (B * S, D))),
        "ctxT": f(np.reshape(a["ctx_1024"], (B * S, D)).T),
        "gateT": f(np.asarray(a["L0_ffn_gate_w"]).T),
        "gateupT": f(np.transpose(a["L0_ffn_gate_up_proj"], (0, 2, 1))),
        "downT": f(np.transpose(a["L0_ffn_down_proj"], (0, 2, 1))),
        "mask": f(np.reshape(a["mask_BxSxS2_if1"], (B * S, S))),
        "maskT": f(np.reshape(np.transpose(a["mask_BxSxS2_if1"], (0, 2, 1)), (B * S, S))),
        "wqT": f(np.asarray(a["L1_xattn_Wq"]).T), "bq": f(a["L1_xattn_bq"]),
        "wkT": f(np.asarray(a["L1_xattn_Wk"]).T), "bk": f(a["L1_xattn_bk"]),
        "wvT": f(np.asarray(a["L1_xattn_Wv"]).T), "bv": f(a["L1_xattn_bv"]),
        "sWq": f(a["L1_ffn_Wq"]), "sWk": f(np.asarray(a["L1_ffn_Wkv"])[:, :SH * SDK]),
        "sWv": f(np.asarray(a["L1_ffn_Wkv"])[:, SH * SDK:]), "sWs": f(a["L1_ffn_Ws"]),
        "sWo": f(np.reshape(a["L1_ffn_Wo"], (SH * SDK, D))), "sbo": f(a["L1_ffn_bo"]),
        "woT": cross_output_rows(a["L1_xattn_Wo"], a["L1_xattn_bo"]),
    }


def kernel(**inputs):
    import numpy as np
    import concourse.bacc as bacc
    from concourse.bass_utils import run_bass_kernel_spmd

    nc = bacc.Bacc("TRN2", target_bir_lowering=False, num_devices=1)
    arrays = layout({name: np.asarray(v) for name, v in inputs.items()})
    io = {name: nc.dram_tensor(name, v.shape, mybir.dt.from_np(v.dtype), kind="ExternalInput").ap() for name, v in arrays.items()}
    io["out"] = nc.dram_tensor("out", (B * S, D), F32, kind="ExternalOutput").ap()
    build(nc, io)
    result = run_bass_kernel_spmd(nc, [arrays], core_ids=[0])
    return result.results[0]["out"].reshape(B, S, D)
```

```python
from contextlib import ExitStack

import concourse.bass as bass
from concourse import mybir

ALU = mybir.AluOpType
ACT = mybir.ActivationFunctionType
AX = mybir.AxisListType
F32 = mybir.dt.float32
BF16 = mybir.dt.bfloat16
F32R = mybir.dt.float32r
I32 = mybir.dt.int32
U32 = mybir.dt.uint32

P = 128
B, S, D = 8, 512, 256
KC = D // P
TB = S // P
NT = B * TB
E, F = 8, 1024
FC = F // P
TOPK = 2
MAXT = NT * TOPK + E - 1
EPS = 1e-5
HEADS, DK = 16, 16
G, HG = 4, 4
SH, SDK, STOP = 8, 64, 3
MASKED = -2.0 ** 32


class Names:

    def __init__(self, nc, ctx, tag):
        self.nc, self.ctx, self.tag = nc, ctx, tag

    def sb(self, name, shape, dt=F32):
        return self.ctx.enter_context(self.nc.sbuf_tensor(f"{self.tag}_{name}", shape, dt))

    def ps(self, name, shape, dt=F32):
        return self.ctx.enter_context(self.nc.psum_tensor(f"{self.tag}_{name}", shape, dt))

    def sem(self, name):
        return self.ctx.enter_context(self.nc.semaphore(f"{self.tag}_{name}"))


def constants(nc, ident, before, ones, iota8):
    with ExitStack() as ctx:
        m = Names(nc, ctx, "const")
        filled, done = m.sem("filled"), m.sem("done")
        block = ctx.enter_context(nc.Block())

        @block.gpsimd
        def _(pool):
            pool.memset(ident[:, :], 0.0).then_inc(filled, 1)
            pool.memset(before[:, :], 0.0).then_inc(filled, 1)
            pool.memset(ones[:, :], 1.0).then_inc(done, 1)
            for e in range(E):
                pool.memset(iota8[:, e:e + 1], float(e)).then_inc(done, 1)
            pool.wait_ge(filled, 2)
            pool.affine_select(out=ident[:, :], in_=ident[:, :], compare_op=ALU.not_equal, fill=1.0,
                               base=0, pattern=[[-1, P]], channel_multiplier=1).then_inc(done, 1)
            pool.affine_select(out=before[:, :], in_=before[:, :], compare_op=ALU.is_ge, fill=1.0,
                               base=0, pattern=[[-1, P]], channel_multiplier=1).then_inc(done, 1)
            pool.wait_ge(done, E + 3)


def rstd_steps(act, dve, *, var, std, rstd, eps, stats_ready, std_ready, rstd_ready):
    if act is not None:
        act.wait_ge(stats_ready, 1)
        act.activation(std, var, ACT.Sqrt, bias=eps).then_inc(std_ready, 1)
    if dve is not None:
        dve.wait_ge(std_ready, 1)
        dve.reciprocal(rstd, std).then_inc(rstd_ready, 1)


def feature_attention(nc, x_in, ctxT_in, x, stats, ident):
    with ExitStack() as ctx:
        m = Names(nc, ctx, "fa")
        st6 = m.sb("st6", [P, NT, 6])
        mv = m.sb("mv", [P, NT, 2])
        std = m.sb("std", [P, NT])
        rstd = m.sb("rstd", [P, NT])
        eps = m.sb("eps", [P, 1])
        ctxT = m.sb("ctxT", [P, KC, B * S])
        gq = m.sb("gq", [P, KC, B * S])
        xn = m.sb("xn", [P, TB, D])
        gk = m.sb("gk", [P, KC, S])
        k1 = m.sb("k1", [P, KC, S])
        junk = m.sb("junk", [P, KC, S])
        qk = m.sb("qk", [P, KC, 1])
        ex = m.sb("ex", [P, KC, S])
        at = m.sb("at", [P, 2, KC, S])
        negmax = m.sb("negmax", [P, KC * B])
        esum = m.sb("esum", [P, KC])
        rsum = m.sb("rsum", [P, KC])
        xnT = m.ps("xnT", [P, KC, S])
        att = [m.ps(f"att{i}", [P, TB, D]) for i in range(2)]

        x_in_done = [m.sem(f"x_in{i}") for i in range(4)]
        ctx_in = m.sem("ctx_in")
        eps_set = m.sem("eps_set")
        st_done = m.sem("st_done")
        stats_ready, std_ready, rstd_ready = m.sem("stats_ready"), m.sem("std_ready"), m.sem("rstd_ready")
        xn_ready, xnT_ready = m.sem("xn_ready"), m.sem("xnT_ready")
        gq_ready, gk_ready, k1_ready = m.sem("gq_ready"), m.sem("gk_ready"), m.sem("k1_ready")
        qk_ready, qks_ready, en_ready = m.sem("qk_ready"), m.sem("qks_ready"), m.sem("en_ready")
        mx_ready = m.sem("mx_ready")
        ex_ready, rs_ready, at_ready, att_ready = m.sem("ex_ready"), m.sem("rs_ready"), m.sem("at_ready"), m.sem("att_ready")
        x_added, st2_done = m.sem("x_added"), m.sem("st2_done")
        block = ctx.enter_context(nc.Block())
        xv = x_in.rearrange("(t p) d -> p t d", p=P)

        @block.sync
        def _(sp):
            for i in range(4):
                sp.dma_start(x[:, i * TB * 2:(i + 1) * TB * 2, :], xv[:, i * TB * 2:(i + 1) * TB * 2, :]).then_inc(x_in_done[i], 16)
            sp.dma_start(ctxT[:, :, :], ctxT_in.rearrange("(c p) n -> p c n", p=P)).then_inc(ctx_in, 16)

        @block.tensor
        def _(pe):
            with pe.Fori(0, B) as b:
                pe.wait_ge(xn_ready, (b + 1) * TB)
                pe.wait_ge(gq_ready, b + 1)
                for i in range(TB):
                    for c in range(KC):
                        last = pe.transpose(xnT[:, c, i * P:(i + 1) * P], xn[:, i, c * P:(c + 1) * P], ident[:, :])
                last.then_inc(xnT_ready, 1)
            with pe.Fori(0, B // 2) as half:
                for par in range(2):
                    b = half * 2 + par
                    pe.wait_ge(at_ready, b * KC + (KC + 1))
                    pe.wait_ge(x_added, b + 1)
                    for i in range(TB):
                        for c in range(KC):
                            last = pe.transpose(att[par][:, i, c * P:(c + 1) * P], at[:, par, c, i * P:(i + 1) * P], ident[:, :])
                    last.then_inc(att_ready, 1)

        @block.scalar
        def _(act):
            act.wait_ge(eps_set, 1)
            rstd_steps(act, None, var=mv[:, :, 1], std=std[:, :], rstd=None, eps=eps[:, 0:1],
                       stats_ready=stats_ready, std_ready=std_ready, rstd_ready=None)
            act.activation(junk[:, 0, 0:1], eps[:, 0:1], ACT.Gelu).then_inc(gq_ready, 1)
            act.wait_ge(ctx_in, 16)
            with act.Fori(0, B) as b:
                act.wait_ge(k1_ready, b + 1)
                act.activation(gk[:, :, :], ctxT[:, :, bass.ts(b, S)], ACT.Gelu).then_inc(gk_ready, 1)
                act.wait_ge(xnT_ready, b + 1)
                act.activation(gq[:, :, bass.ts(b, S)], xnT[:, :, :], ACT.Gelu).then_inc(gq_ready, 1)
            act.wait_ge(mx_ready, B)
            with act.Fori(0, B) as b:
                act.wait_ge(at_ready, b * KC + 1)
                for c in range(KC):
                    act.activation(ex[:, c, :], gq[:, c, bass.ts(b, S)], ACT.Exp,
                                   bias=negmax[:, bass.ds(b * KC + c, 1)], accum_out=esum[:, c:c + 1]).then_inc(ex_ready, 1)

        @block.vector
        def _(dve):
            dve.memset(eps[:, :], EPS).then_inc(eps_set, 1)
            for t in range(NT):
                if t % (TB * 2) == 0:
                    dve.wait_ge(x_in_done[t // (TB * 2)], 16)
                dve.bn_stats(st6[:, t, :], x[:, t, :]).then_inc(st_done, 1)
            for t in range(NT):
                if t in (0, NT // 2):
                    dve.wait_ge(st_done, NT)
                last = dve.bn_aggr(mv[:, t, :], st6[:, t, :])
            last.then_inc(stats_ready, 1)
            rstd_steps(None, dve, var=None, std=std[:, :], rstd=rstd[:, :], eps=None,
                       stats_ready=None, std_ready=std_ready, rstd_ready=rstd_ready)
            dve.wait_ge(rstd_ready, 1)
            dve.memset(k1[:, :, :], 0.0).then_inc(k1_ready, 1)

            def normalise(tile):
                for i in range(TB):
                    t = tile + i
                    dve.tensor_scalar(xn[:, i, :], x[:, bass.ds(t, 1), :], mv[:, bass.ds(t, 1), 0],
                                      rstd[:, bass.ds(t, 1)], ALU.subtract, ALU.mult).then_inc(xn_ready, 1)

            normalise(0)
            with dve.Fori(0, B) as b:
                dve.wait_ge(xnT_ready, b + 1)
                normalise(((b + 1) % B) * TB)
                dve.wait_ge(gk_ready, b + 1)
                dve.tensor_scalar(k1[:, :, :], gk[:, :, :], 1.0, None, ALU.add).then_inc(k1_ready, 1)
                dve.wait_ge(k1_ready, b + 2)
                dve.wait_ge(gq_ready, b + 2)
                for c in range(KC):
                    dve.scalar_tensor_tensor(out=junk[:, c, :], in0=gq[:, c, bass.ts(b, S)], scalar=1.0, in1=k1[:, c, :],
                                             op0=ALU.add, op1=ALU.mult, accum_out=qk[:, c, :]).then_inc(qk_ready, 1)
                dve.wait_ge(qk_ready, (b + 1) * KC)
                dve.tensor_scalar(qk[:, :, :], qk[:, :, :], 1.0 / D ** 0.5, None, ALU.mult).then_inc(qks_ready, 1)
                dve.wait_ge(qks_ready, b + 1)
                for c in range(KC):
                    dve.tensor_scalar(gq[:, c, bass.ts(b, S)], gq[:, c, bass.ts(b, S)], 1.0, qk[:, c, :],
                                      ALU.add, ALU.mult).then_inc(en_ready, 1)
                dve.wait_ge(en_ready, (b + 1) * KC)
                dve.tensor_reduce(negmax[:, bass.ds(b * KC, KC)], gq[:, :, bass.ts(b, S)], AX.X, ALU.max,
                                  negate=True).then_inc(mx_ready, 1)
            dve.memset(rsum[:, :], 0.0).then_inc(at_ready, 1)
            dve.wait_ge(at_ready, 1)
            for i in range(2):
                dve.memset(junk[:, 0, i:i + 1], 0.0).then_inc(x_added, 1)

            def attend(b, par):
                dve.wait_ge(ex_ready, b * KC + KC)
                dve.reciprocal(rsum[:, :], esum[:, :]).then_inc(rs_ready, 1)
                dve.wait_ge(rs_ready, b + 1)
                for c in range(KC):
                    dve.scalar_tensor_tensor(out=at[:, par, c, :], in0=ex[:, c, :], scalar=rsum[:, c:c + 1],
                                             in1=ctxT[:, c, bass.ds(b * S, S)], op0=ALU.mult, op1=ALU.mult).then_inc(at_ready, 1)

            def add(b, par):
                dve.wait_ge(att_ready, b + 1)
                dve.tensor_tensor(x[:, bass.ds(b * TB, TB), :], att[par][:, :, :], x[:, bass.ds(b * TB, TB), :], ALU.add).then_inc(x_added, 1)
                dve.wait_ge(x_added, b + 3)
                for i in range(TB):
                    dve.bn_stats(stats[:, bass.ds(b * TB + i, 1), :], x[:, bass.ds(b * TB + i, 1), :]).then_inc(st2_done, 1)

            attend(0, 0)
            with dve.Fori(0, B // 2 - 1) as half:
                for par in range(2):
                    attend(half * 2 + (par + 1), 1 - par)
                    add(half * 2 + par, par)
            attend(B - 1, 1)
            add(B - 2, 0)
            add(B - 1, 1)
            dve.wait_ge(st2_done, NT)


def load_expert(queue, io, e, gu_w, dn_w, w_in):
    queue.dma_start(gu_w[e % 2][:, :, :], io["gateupT"][e].rearrange("(c p) f -> p c f", p=P)).then_inc(w_in[e % 2], 16)
    queue.dma_start(dn_w[e % 2][:, :, :], io["downT"][e].rearrange("(c p) d -> p c d", p=P)).then_inc(w_in[e % 2], 16)


def route(nc, io, rows, outs, x, stats, ident, before, ones, iota8, xn, weight, place, tile_at, gu_w, dn_w, w_in):
    with ExitStack() as ctx:
        m = Names(nc, ctx, "rt")
        mv = m.sb("mv", [P, NT, 2])
        std, rstd, eps = m.sb("std", [P, NT]), m.sb("rstd", [P, NT]), m.sb("eps", [P, 1])
        zeros = m.sb("zeros", [P, 4 * D])
        gateT = m.sb("gateT", [P, KC, E])
        xt = m.sb("xt", [P, 2, KC, P])
        logit = m.sb("logit", [P, NT, E])
        top = m.sb("top", [P, NT, 8])
        topi = m.sb("topi", [P, NT, 8], U32)
        topf = m.sb("topf", [P, NT, 8])
        hot = m.sb("hot", [P, TOPK, NT, E])
        both = m.sb("both", [P, NT, E])
        scan = m.sb("scan", [P, 2, NT, E])
        counts = m.sb("counts", [P, E])
        tiles_i = m.sb("tiles_i", [P, E], I32)
        tiles_f = m.sb("tiles_f", [P, E])
        start = m.sb("start", [P, E + 1])
        pos = m.sb("pos", [P, NT, E])
        picked = m.sb("picked", [P, TOPK, NT, E])
        placef = m.sb("placef", [P, TOPK, NT])
        wtmp = m.sb("wtmp", [P, 3, NT])
        xtp = [m.ps(f"xtp{i}", [P, KC, P]) for i in range(2)]
        lg = m.ps("lg", [P, NT, E])
        inside = m.ps("inside", [P, NT, E])
        total = m.ps("total", [P, NT, E])

        gate_in, zero_set, zeroed = m.sem("gate_in"), m.sem("zero_set"), m.sem("zeroed")
        aggr, eps_set, stats_ready, std_ready, rstd_ready = (m.sem("aggr"), m.sem("eps_set"), m.sem("stats_ready"),
                                                             m.sem("std_ready"), m.sem("rstd_ready"))
        xn_ready, xtp_ready, xt_ready, lg_ready, lg_out = (m.sem("xn_ready"), m.sem("xtp_ready"), m.sem("xt_ready"),
                                                           m.sem("lg_ready"), m.sem("lg_out"))
        both_ready, sums_ready, diff_ready, exp_ready, placed, scattered = (
            m.sem("both_ready"), m.sem("sums_ready"), m.sem("diff_ready"), m.sem("exp_ready"), m.sem("placed"), m.sem("scattered"))
        step, spare_zeroed = m.sem("step"), m.sem("spare_zeroed")
        block = ctx.enter_context(nc.Block())

        @block.sync
        def _(sp):
            sp.dma_start(gateT[:, :, :], io["gateT"].rearrange("(c p) e -> p c e", p=P)).then_inc(gate_in, 16)
            sp.wait_ge(zero_set, 1)
            per = rows.shape[0] // (4 * P)
            for i in range(per):
                sp.dma_start(rows[i * 4 * P:(i + 1) * 4 * P, :].rearrange("(p r) d -> p (r d)", p=P), zeros[:, :]).then_inc(zeroed, 16)
            sp.dma_start(outs[NT * TOPK * P:MAXT * P, :].rearrange("(p r) d -> p r d", p=P),
                         zeros[:, 0:D].rearrange("p (a d) -> p a d", a=1).to_broadcast([P, MAXT - NT * TOPK, D])).then_inc(spare_zeroed, 16)
            sp.wait_ge(zeroed, 16 * per)
            sp.wait_ge(spare_zeroed, 16)

        def gate_tile(pe, t):
            pe.wait_ge(xt_ready, t + 1)
            for c in range(KC):
                last = pe.matmul(lg[:, t, :], xt[:, t % 2, c, :], gateT[:, c, :], start=(c == 0), stop=(c == KC - 1))
            last.then_inc(lg_ready, 1)

        @block.tensor
        def _(pe):
            pe.wait_ge(gate_in, 16)
            for t in range(NT):
                pe.wait_ge(xn_ready, t + 1)
                if t >= 2:
                    pe.wait_ge(xt_ready, t - 1)
                for c in range(KC):
                    last = pe.transpose(xtp[t % 2][:, c, :], xn[:, t, c * P:(c + 1) * P], ident[:, :])
                last.then_inc(xtp_ready, 1)
                if t >= 1:
                    gate_tile(pe, t - 1)
            gate_tile(pe, NT - 1)
            pe.wait_ge(both_ready, 1)
            pe.matmul(inside[:, :, :], before[:, :], both[:, :, :], start=True, stop=True).then_inc(sums_ready, 1)
            pe.matmul(total[:, :, :], ones[:, :], both[:, :, :], start=True, stop=True).then_inc(sums_ready, 1)

        @block.scalar
        def _(act):
            act.wait_ge(eps_set, 1)
            rstd_steps(act, None, var=mv[:, :, 1], std=std[:, :], rstd=None, eps=eps[:, 0:1],
                       stats_ready=stats_ready, std_ready=std_ready, rstd_ready=None)
            for t in range(NT):
                act.wait_ge(xtp_ready, t + 1)
                if t >= 2:
                    act.wait_ge(lg_ready, t - 1)
                act.copy(xt[:, t % 2, :, :], xtp[t % 2][:, :, :]).then_inc(xt_ready, 1)
            act.wait_ge(diff_ready, 1)
            act.activation(wtmp[:, 1, :], wtmp[:, 0, :], ACT.Exp).then_inc(exp_ready, 1)

        @block.gpsimd
        def _(pool):
            pool.memset(zeros[:, :], 0.0).then_inc(zero_set, 1)
            for e in range(2):
                load_expert(pool, io, e, gu_w, dn_w, w_in)
            pool.wait_ge(placed, 1)
            pool.wait_ge(zeroed, 16 * (rows.shape[0] // (4 * P)))
            for t in range(NT):
                for j in range(TOPK):
                    pool.indirect_dma_start(rows, bass.IndirectOffsetOnAxis(ap=place[:, j, t:t + 1], axis=0),
                                            xn[:, t, :], None).then_inc(scattered, 16)
            pool.wait_ge(scattered, 16 * NT * TOPK)

        @block.vector
        def _(dve):
            n = [0]

            def then(ins):
                n[0] += 1
                ins.then_inc(step, 1)
                dve.wait_ge(step, n[0])

            dve.memset(eps[:, :], EPS).then_inc(eps_set, 1)
            for t in range(NT):
                last = dve.bn_aggr(mv[:, t, :], stats[:, t, :])
            last.then_inc(stats_ready, 1)
            rstd_steps(None, dve, var=None, std=std[:, :], rstd=rstd[:, :], eps=None,
                       stats_ready=None, std_ready=std_ready, rstd_ready=rstd_ready)
            dve.wait_ge(rstd_ready, 1)
            for t in range(NT):
                dve.tensor_scalar(xn[:, t, :], x[:, t, :], mv[:, t, 0:1], rstd[:, t:t + 1],
                                  ALU.subtract, ALU.mult).then_inc(xn_ready, 1)
            dve.wait_ge(lg_ready, NT)
            dve.tensor_copy(logit[:, :, :], lg[:, :, :]).then_inc(lg_out, 1)
            dve.wait_ge(lg_out, 1)
            for t in range(NT):
                last = dve.max(top[:, t, :], logit[:, t, :])
            then(last)
            for t in range(NT):
                last = dve.max_index(topi[:, t, :], top[:, t, :], logit[:, t, :])
            then(last)
            then(dve.tensor_copy(topf[:, :, :], topi[:, :, :]))
            experts = iota8[:, :].rearrange("p (a e) -> p a e", a=1).to_broadcast([P, NT, E])
            for j in range(TOPK):
                ins = dve.tensor_tensor(hot[:, j, :, :], topf[:, :, j:j + 1].to_broadcast([P, NT, E]), experts, ALU.is_equal)
            then(ins)
            dve.tensor_tensor(both[:, :, :], hot[:, 0, :, :], hot[:, 1, :, :], ALU.add).then_inc(both_ready, 1)
            dve.tensor_tensor(wtmp[:, 0, :], top[:, :, 1], top[:, :, 0], ALU.subtract).then_inc(diff_ready, 1)
            dve.wait_ge(exp_ready, 1)
            then(dve.tensor_scalar(wtmp[:, 2, :], wtmp[:, 1, :], 1.0, None, ALU.add))
            then(dve.reciprocal(weight[:, 0, :], wtmp[:, 2, :]))
            then(dve.tensor_tensor(weight[:, 1, :], wtmp[:, 1, :], weight[:, 0, :], ALU.mult))
            dve.wait_ge(sums_ready, 2)
            dve.memset(scan[:, 0, 0:1, :], 0.0)
            then(dve.tensor_copy(scan[:, 0, 1:NT, :], total[:, 0:NT - 1, :]))
            src, d = 0, 1
            while d < NT:
                dve.tensor_copy(scan[:, 1 - src, 0:d, :], scan[:, src, 0:d, :])
                then(dve.tensor_tensor(scan[:, 1 - src, d:NT, :], scan[:, src, d:NT, :], scan[:, src, 0:NT - d, :], ALU.add))
                src, d = 1 - src, 2 * d
            then(dve.tensor_tensor(counts[:, :], total[:, NT - 1, :], scan[:, src, NT - 1, :], ALU.add))
            then(dve.tensor_scalar(counts[:, :], counts[:, :], 1.0, float(P - 1), ALU.max, ALU.add))
            then(dve.tensor_copy(tiles_i[:, :], counts[:, :]))
            then(dve.tensor_scalar(tiles_i[:, :], tiles_i[:, :], 7, None, ALU.arith_shift_right))
            then(dve.tensor_copy(tiles_f[:, :], tiles_i[:, :]))
            then(dve.memset(start[:, 0:1], 0.0))
            for e in range(E):
                then(dve.tensor_tensor(start[:, e + 1:e + 2], start[:, e:e + 1], tiles_f[:, e:e + 1], ALU.add))
            dve.tensor_copy(tile_at[:, :], start[:, :])
            then(dve.tensor_tensor(pos[:, :, :], inside[:, :, :], scan[:, src, :, :], ALU.add))
            then(dve.tensor_scalar(start[:, :], start[:, :], float(P), None, ALU.mult))
            first = start[:, 0:E].rearrange("p (a e) -> p a e", a=1).to_broadcast([P, NT, E])
            then(dve.tensor_tensor(pos[:, :, :], pos[:, :, :], first, ALU.add))
            for j in range(TOPK):
                ins = dve.tensor_tensor(picked[:, j, :, :], hot[:, j, :, :], pos[:, :, :], ALU.mult)
            then(ins)
            then(dve.tensor_reduce(placef[:, :, :], picked[:, :, :, :], AX.X, ALU.add))
            dve.tensor_copy(place[:, :, :], placef[:, :, :]).then_inc(placed, 1)


def experts(nc, io, rows, outs, ident, ones, tile_at, bias, flag, gu_w, dn_w, w_in):
    with ExitStack() as ctx:
        m = Names(nc, ctx, "ex")
        xin = m.sb("xin", [P, D])
        xt = m.sb("xt", [P, KC, P])
        sg = m.sb("sg", [P, 2, FC // 2, P])
        h = m.sb("h", [P, FC, P])
        y = m.sb("y", [P, D])
        xtp = m.ps("xtp", [P, KC, P])
        gp = [m.ps(f"gp{i}", [P, FC // 2, P]) for i in range(2)]
        up = [m.ps(f"up{i}", [P, FC // 2, P]) for i in range(2)]
        yp = m.ps("yp", [P, D])
        mark = m.ps("mark", [P, P])
        raw, made = m.sb("raw", [P, S], I32), m.sb("made", [P, S], BF16)
        least, lowest = m.sb("least", [P, S]), m.sb("lowest", [P, 1])
        summed = m.ps("summed", [P, 1])
        raw_in, made_ready, least_ready, bias_stored, lowest_ready, summed_ready, flag_ready = (
            m.sem(n) for n in ("raw_in", "made_ready", "least_ready", "bias_stored", "lowest_ready", "summed_ready", "flag_ready"))
        expert_done = m.sem("expert_done")
        x_in, xtp_ready, xt_ready, g_ready, s_ready, u_ready, h_ready, yp_ready, y_ready, stored = (
            m.sem(n) for n in ("x_in", "xtp_ready", "xt_ready", "g_ready", "s_ready", "u_ready", "h_ready", "yp_ready", "y_ready", "stored"))
        block = ctx.enter_context(nc.Block())
        HC = FC // 2
        PIECES = 2 * B * S // P

        def bound(eng, e):
            return eng.value_load(tile_at[0:1, e:e + 1], min_val=1 if e else 0, max_val=MAXT)

        @block.sync
        def _(sp):
            total = bound(sp, E)
            with sp.Fori(0, sp.snap(total + 1)) as g:
                sp.wait_ge(xtp_ready, g + 1)
                sp.dma_start(xin[:, :], rows[bass.ts(g, P), :]).then_inc(x_in, 16)

        @block.gpsimd
        def _(pool):
            for e in range(2, E):
                pool.wait_ge(expert_done, e - 1)
                load_expert(pool, io, e, gu_w, dn_w, w_in)

        @block.tensor
        def _(pe):
            def turn():
                for c in range(KC):
                    last = pe.transpose(xtp[:, c, :], xin[:, c * P:(c + 1) * P], ident[:, :])
                last.then_inc(xtp_ready, 1)

            pe.transpose(xtp[:, 0, :], ident[:, :], ident[:, :]).then_inc(xtp_ready, 1)
            pe.wait_ge(x_in, 16)
            turn()
            for e in range(E):
                pe.wait_ge(w_in[e % 2], 32 * (e // 2 + 1))
                with pe.Fori(bound(pe, e), bound(pe, e + 1)) as g:
                    pe.wait_ge(xt_ready, g + 1)
                    for i in range(2):
                        for w, out, done in ((0, gp[i], g_ready), (F, up[i], u_ready)):
                            for f in range(HC):
                                col = w + (i * HC + f) * P
                                for c in range(KC):
                                    last = pe.matmul(out[:, f, :], gu_w[e % 2][:, c, col:col + P], xt[:, c, :],
                                                     start=(c == 0), stop=(c == KC - 1))
                            last.then_inc(done, 1)
                    pe.wait_ge(x_in, g * 16 + 32)
                    turn()
                    pe.wait_ge(y_ready, g + 1)
                    for i in range(2):
                        pe.wait_ge(h_ready, 2 * g + i + 1)
                        for f in range(i * HC, (i + 1) * HC):
                            last = pe.matmul(yp[:, :], h[:, f, :], dn_w[e % 2][:, f, :], start=(f == 0), stop=(f == FC - 1))
                    last.then_inc(yp_ready, 1)
                pe.transpose(mark[:, :], ident[:, :], ident[:, :]).then_inc(expert_done, 1)
            pe.wait_ge(lowest_ready, 1)
            pe.matmul(summed[:, :], ones[:, :], lowest[:, :], start=True, stop=True).then_inc(summed_ready, 1)

        @block.scalar
        def _(act):
            act.copy(y[:, 0:P], ident[:, :]).then_inc(y_ready, 1)
            act.wait_ge(y_ready, 1)
            act.dma_start(outs[0:P, 0:P], y[:, 0:P]).then_inc(stored, 16)
            act.wait_ge(made_ready, 1)
            act.dma_start(bias[0:P, :], made[:, :]).then_inc(bias_stored, 16)
            tiles = bound(act, E)
            with act.Fori(0, tiles) as g:
                act.wait_ge(made_ready, g + 1)
                act.dma_start(raw[:, :], io["masks"][bass.ds((g % PIECES) * P, P), :]).then_inc(raw_in, 16)
                for i in range(2):
                    act.wait_ge(g_ready, 2 * g + i + 1)
                    act.activation(sg[:, i, :, :], gp[i][:, :, :], ACT.Silu).then_inc(s_ready, 1)
                act.wait_ge(stored, g * 16 + 16)
                act.wait_ge(yp_ready, g + 1)
                act.copy(y[:, :], yp[:, :]).then_inc(y_ready, 1)
                act.wait_ge(y_ready, g + 2)
                act.dma_start(outs[bass.ts(g, P), :], y[:, :]).then_inc(stored, 16)
                act.wait_ge(made_ready, g + 2)
                act.dma_start(bias[bass.ds((g % PIECES) * P, P), :], made[:, :]).then_inc(bias_stored, 16)
            act.wait_ge(stored, tiles * 16 + 16)
            act.wait_ge(bias_stored, tiles * 16 + 16)
            act.copy(y[:, 0:1], ident[:, 0:1])

        @block.vector
        def _(dve):
            dve.wait_ge(xtp_ready, 2)
            dve.tensor_copy(xt[:, :, :], xtp[:, :, :]).then_inc(xt_ready, 1)
            dve.memset(least[:, :], 0.0).then_inc(least_ready, 1)
            dve.memset(made[:, :], 0.0).then_inc(made_ready, 1)
            with dve.Fori(0, bound(dve, E)) as g:
                for i in range(2):
                    dve.wait_ge(u_ready, 2 * g + i + 1)
                    dve.wait_ge(s_ready, 2 * g + i + 1)
                    dve.tensor_tensor(h[:, i * HC:(i + 1) * HC, :], up[i][:, :, :], sg[:, i, :, :], ALU.mult).then_inc(h_ready, 1)
                dve.wait_ge(xtp_ready, g + 3)
                dve.tensor_copy(xt[:, :, :], xtp[:, :, :]).then_inc(xt_ready, 1)
                dve.wait_ge(raw_in, g * 16 + 16)
                dve.wait_ge(bias_stored, g * 16 + 16)
                dve.wait_ge(least_ready, g + 1)
                dve.tensor_scalar(made[:, :], raw[:, :], 0.0, MASKED, ALU.is_equal, ALU.mult).then_inc(made_ready, 1)
                dve.wait_ge(made_ready, g + 2)
                dve.tensor_tensor(least[:, :], least[:, :], made[:, :], ALU.min).then_inc(least_ready, 1)
            tiles = bound(dve, E)
            dve.wait_ge(least_ready, tiles + 1)
            dve.tensor_reduce(lowest[:, :], least[:, :], AX.X, ALU.min).then_inc(lowest_ready, 1)
            dve.wait_ge(summed_ready, 1)
            dve.tensor_scalar(flag[:, :], summed[:, :], 0.0, None, ALU.is_lt).then_inc(flag_ready, 1)


def load_context(queue, io, ctxT, ctx_in, b):
    queue.dma_start(ctxT[:, :, :], io["ctxT"].rearrange("(c p) n -> p c n", p=P)[:, :, bass.ds(b * S, S)]).then_inc(ctx_in, 16)


def combine(nc, io, outs, x, weight, place, mv, rstd, weights, ctxT, w_in, ctx_in):
    with ExitStack() as ctx:
        m = Names(nc, ctx, "cb")
        got = m.sb("got", [P, NT, TOPK, D])
        st6, std, eps = m.sb("st6", [P, NT, 6]), m.sb("std", [P, NT]), m.sb("eps", [P, 1])
        gathered = [m.sem(f"gathered{i}") for i in range(8)]
        added, eps_set = m.sem("added"), m.sem("eps_set")
        st_ready, stats_ready, std_ready, rstd_ready = (m.sem(n) for n in ("st_ready", "stats_ready", "std_ready", "rstd_ready"))
        block = ctx.enter_context(nc.Block())
        Q = NT // 8

        @block.sync
        def _(sp):
            for name in ("wq", "wk", "wv"):
                sp.dma_start(weights[name][:, :, :], io[name + "T"].rearrange("(c p) n -> p c n", p=P)).then_inc(w_in, 16)
            load_context(sp, io, ctxT, ctx_in, 0)
            sp.dma_start(weights["wo"][:, :, :], io["woT"].rearrange("(g p) n -> p g n", p=P)).then_inc(w_in, 16)
            for name in ("bq", "bk"):
                sp.dma_start(weights[name][:, :], io[name].rearrange("(c p) -> p c", p=P), allow_slow_non_contiguous=True).then_inc(w_in, 16)
            sp.dma_start(weights["bv"][:, :], io["bv"].rearrange("(a n) -> a n", a=1).to_broadcast([P, D])).then_inc(w_in, 16)

        @block.gpsimd
        def _(pool):
            for t in range(NT):
                for j in range(TOPK):
                    pool.indirect_dma_start(got[:, t, j, :], None, outs,
                                            bass.IndirectOffsetOnAxis(ap=place[:, j, t:t + 1], axis=0)).then_inc(gathered[t // Q], 16)

        @block.scalar
        def _(act):
            act.wait_ge(eps_set, 1)
            rstd_steps(act, None, var=mv[:, :, 1], std=std[:, :], rstd=None, eps=eps[:, 0:1],
                       stats_ready=stats_ready, std_ready=std_ready, rstd_ready=None)

        @block.vector
        def _(dve):
            dve.memset(eps[:, :], EPS).then_inc(eps_set, 1)
            for q in range(8):
                dve.wait_ge(gathered[q], 16 * Q * TOPK)
                for j in range(TOPK):
                    for i in range(Q):
                        t = q * Q + i
                        if j:
                            dve.wait_ge(added, q * Q * TOPK + i + 1)
                        dve.scalar_tensor_tensor(out=x[:, t, :], in0=got[:, t, j, :], scalar=weight[:, j, t:t + 1],
                                                 in1=x[:, t, :], op0=ALU.mult, op1=ALU.add).then_inc(added, 1)
                for i in range(Q):
                    t = q * Q + i
                    dve.wait_ge(added, q * Q * TOPK + Q + i + 1)
                    dve.bn_stats(st6[:, t, :], x[:, t, :]).then_inc(st_ready, 1)
                for i in range(Q):
                    t = q * Q + i
                    dve.wait_ge(st_ready, t + 1)
                    last = dve.bn_aggr(mv[:, t, :], st6[:, t, :])
            last.then_inc(stats_ready, 1)
            rstd_steps(None, dve, var=None, std=std[:, :], rstd=rstd[:, :], eps=None,
                       stats_ready=None, std_ready=std_ready, rstd_ready=rstd_ready)
            dve.wait_ge(rstd_ready, 1)


def cross_attention(nc, io, x, mv, rstd, ident, ones, bias, flag, q_parts, k_parts, weights, ctxT, w_in, ctx_in):
    with ExitStack() as ctx:
        m = Names(nc, ctx, "ca")
        R4 = 4 * DK
        wq, wk, wv, wo, bq, bk, bv = (weights[n] for n in ("wq", "wk", "wv", "wo", "bq", "bk", "bv"))
        ident16, tiny16 = m.sb("ident16", [P, P], BF16), m.sb("tiny16", [P, P], BF16)
        xn, xT = m.sb("xn", [P, TB, D]), m.sb("xT", [P, KC, S])
        nb, nbT = m.sb("nb", [P, 2, TB, S], BF16), m.sb("nbT", [P, 2, TB, S], BF16)
        rv = m.sb("rv", [P, S])
        qf = m.sb("qf", [P, KC, S])
        qp, kp = m.sb("qp", [P, 2, KC, S], F32R), m.sb("kp", [P, 2, KC, S], F32R)
        q_stack = [m.sb(f"q_stack{g}", [P, HG, S], F32R) for g in range(G)]
        k_stack = [m.sb(f"k_stack{g}", [P, HG, S], F32R) for g in range(G)]
        negmax = m.sb("negmax", [P, 2, TB, HG])
        zrow = m.sb("zrow", [2, P])
        mfull, mrow = m.sb("mfull", [HG, S]), m.sb("mrow", [HG, 2, S], F32R)
        pr = m.sb("pr", [P, 2, HG, S])
        vstage = m.sb("vstage", [P, TB, D])
        vw = m.sb("vw", [P, G, TB, HG, 32])
        avs, sums = m.sb("avs", [P, S]), m.sb("sums", [P, S])
        outT = m.sb("outT", [P, G, S])
        tick = m.sb("tick", [P, 1])
        na = [m.ps(f"na{i}", [P, S]) for i in range(2)]
        st = [m.ps(f"st{i}", [P, 2, S]) for i in range(2)]
        av, misc = m.ps("av", [P, S]), m.ps("misc", [P, S])

        set_up = m.sem("set_up")
        nb_in, nbT_in = m.sem("nb_in"), m.sem("nbT_in")
        xn_ready = m.sem("xn_ready")
        qp_ready = m.sem("qp_ready")
        k_head, q_head = m.sem("k_head"), m.sem("q_head")
        k_stored, q_stored = m.sem("k_stored"), m.sem("q_stored")
        stack_in = [m.sem(f"stack_in{g}") for g in range(G)]
        na_full, max_done, st_full, exp_done = m.sem("na_full"), m.sem("max_done"), m.sem("st_full"), m.sem("exp_done")
        mh_ready, ml_ready, m_in = m.sem("mh_ready"), m.sem("ml_ready"), m.sem("m_in")
        av_done, av_free, vw_ready = m.sem("av_done"), m.sem("av_free"), m.sem("vw_ready")
        sums_ready, rec_ready, outT_ready = m.sem("sums_ready"), m.sem("rec_ready"), m.sem("outT_ready")
        misc_full, misc_free = m.sem("misc_full"), m.sem("misc_free")
        block = ctx.enter_context(nc.Block())

        SETUP = 6 + 2 * G
        LOAD = 16 * 9
        SLOTS = TB * HG
        JOBS = [("m", 0, 0), ("k0", 0, 3), ("k1", 0, 6), ("xT0", 0, 8), ("xT1", 0, 10), ("rv", 0, 12),
                ("q0", 0, 15), ("m", 1, 0), ("q1", 1, 3), ("o0", 1, 9), ("o1", 1, 15), ("m", 2, 1), ("v0", 2, 7),
                ("v1", 2, 13), ("m", 3, 1)]
        PIECES = {"m": 1, "k": 2, "x": 1, "r": 1, "q": 2, "v": 4, "o": 4}
        FIRST = ["k0", "k1", "xT0", "xT1", "rv", "q0", "q1", "v0", "v1", "m"]
        nj, nf = len(JOBS), len(FIRST)

        def jobs_at(g, s):
            return [(n, j[0]) for n, j in enumerate(JOBS) if j[1:] == (g, s)]

        def pieces_at(g, s):
            return [(n, j[0], s - j[2] + PIECES[j[0][0]] - 1) for n, j in enumerate(JOBS)
                    if j[1] == g and 0 <= j[2] - s < PIECES[j[0][0]]]

        def number(name):
            return next(n for n, j in enumerate(JOBS) if j[0] == name)

        def nxt(b):
            return b + 1 if isinstance(b, int) else (b + 1) % B

        @block.sync
        def _(sp):
            def load_bias(b, par):
                sp.dma_start(nb[:, par, :, :], bias[bass.ds(b * S, S), :].rearrange("(t p) n -> p t n", p=P)).then_inc(nb_in, 16)
                sp.dma_start(nbT[:, par, :, :], bias[bass.ds(b * S + B * S, S), :].rearrange("(t p) n -> p t n", p=P)).then_inc(nbT_in, 16)

            def store(parts, dram, ready, stored, count):
                sp.wait_ge(ready, count)
                sp.dma_start(dram.rearrange("r (c p) n -> p r c n", p=P), parts[:, :, :, :].bitcast(F32)).then_inc(stored, 16)

            def load_stack(g):
                h = slice(g * HG * DK, (g + 1) * HG * DK)
                for r in range(4):
                    for stack, dram, part in ((q_stack[g], q_parts, r % 2), (k_stack[g], k_parts, r // 2)):
                        sp.dma_start(stack[r * DK:(r + 1) * DK, :, :].bitcast(F32),
                                     dram[part, h, :].rearrange("(h d) n -> d h n", d=DK)).then_inc(stack_in[g], 16)
                sp.dma_start(q_stack[g][R4:R4 + 2, :, :].bitcast(F32).rearrange("p h (t n) -> p (h t) n", n=P),
                             zrow[:, :].rearrange("p (a n) -> p a n", a=1).to_broadcast([2, HG * TB, P])).then_inc(stack_in[g], 16)

            load_bias(0, 0)
            sp.wait_ge(set_up, SETUP)
            store(kp, k_parts, misc_free, k_stored, FIRST.index("k1") + 1)
            store(qp, q_parts, qp_ready, q_stored, KC)
            sp.wait_ge(k_stored, 16)
            sp.wait_ge(q_stored, 16)
            for g in range(G):
                load_stack(g)
            sp.wait_ge(misc_full, FIRST.index("v1") + 1)
            load_context(sp, io, ctxT, ctx_in, 1)
            with sp.Fori(0, B) as b:
                sp.wait_ge(exp_done, b * 32 + 2)
                for g in range(G):
                    sp.wait_ge(stack_in[g], b * LOAD + LOAD)
                load_bias(nxt(b), (b + 1) % 2)
                store(kp, k_parts, misc_free, k_stored, b * nj + (nf + number("k1") + 1))
                store(qp, q_parts, qp_ready, q_stored, b * KC + 2 * KC)
                for g in range(G):
                    sp.wait_ge(exp_done, b * 32 + (8 * g + 10))
                    if g == 0:
                        sp.wait_ge(k_stored, b * 16 + 32)
                        sp.wait_ge(q_stored, b * 16 + 32)
                    load_stack(g)
                    if g == 2:
                        load_context(sp, io, ctxT, ctx_in, (b + 2) % B)
            for g in range(G):
                sp.wait_ge(stack_in[g], LOAD * (B + 1))
            sp.wait_ge(ctx_in, 16 * (B + 2))
            sp.wait_ge(nb_in, 16 * (B + 1))

        @block.tensor
        def _(pe):
            def bank_free(n):
                if not (isinstance(n, int) and n == 0):
                    pe.wait_ge(misc_free, n)

            def max_rows(n, a, par):
                bank_free(n)
                pe.wait_ge(max_done, a * SLOTS + SLOTS + 2)
                for t in range(TB):
                    last = pe.transpose(misc[0:HG, t * P:(t + 1) * P], negmax[:, par, t, :], ident[:, :])
                last.then_inc(misc_full, 1)

            def output(n, b, c, piece):
                if piece == 0:
                    bank_free(n)
                    pe.wait_ge(outT_ready, b * G + 2)
                t = piece // 2
                for g in range(2 * (piece % 2), 2 * (piece % 2) + 2):
                    tok = (2 * c + t) * P
                    last = pe.matmul(misc[:, t * D:(t + 1) * D], outT[:, g, tok:tok + P], wo[:, g, :],
                                     start=(g == 0), stop=(g == G - 1))
                if piece == 3:
                    last.then_inc(misc_full, 1)

            def prepare(n, name, b, piece):
                if piece == 0:
                    bank_free(n)
                c = int(name[-1]) if name != "rv" else 0
                if name == "rv":
                    pe.wait_ge(nbT_in, b * 16 + 16)
                    for t in range(TB):
                        last = pe.matmul(misc[:, :], tiny16[:, :], nbT[:, b % 2, t, :], start=(t == 0), stop=(t == TB - 1))
                elif name[0] == "k":
                    if piece == 0:
                        pe.wait_ge(ctx_in, b * 16 + 16)
                    last = pe.matmul(misc[:, :], wk[:, piece, c * P:(c + 1) * P], ctxT[:, piece, :], start=(piece == 0), stop=(piece == KC - 1))
                elif name[0] == "x":
                    pe.wait_ge(xn_ready, b * TB + TB)
                    for t in range(TB):
                        last = pe.transpose(misc[:, t * P:(t + 1) * P], xn[:, t, c * P:(c + 1) * P], ident[:, :])
                elif name[0] == "q":
                    last = pe.matmul(misc[:, :], wq[:, piece, c * P:(c + 1) * P], xT[:, piece, :], start=(piece == 0), stop=(piece == KC - 1))
                else:
                    t, i = piece // 2, piece % 2
                    tok = (2 * c + t) * P
                    last = pe.matmul(misc[:, t * D:(t + 1) * D], ctxT[:, i, tok:tok + P], wv[:, i, :], start=(i == 0), stop=(i == KC - 1))
                if piece == PIECES[name[0]] - 1:
                    last.then_inc(misc_full, 1)

            def score_a(g, b, s, a, masked):
                h, t = s // TB, s % TB
                if s == 0:
                    pe.wait_ge(stack_in[g], b * LOAD + LOAD)
                    if masked:
                        pe.wait_ge(nb_in, b * 16 + 16)
                pe.wait_ge(max_done, a * SLOTS + s + 1)
                if masked:
                    pe.matmul(na[s % 2][:, :], ident16[:, :], nb[:, b % 2, t, :], start=True, stop=False)
                pe.matmul(na[s % 2][:, :], q_stack[g][:, h, t * P:(t + 1) * P], k_stack[g][:, h, :],
                          start=not masked, stop=True).then_inc(na_full, 1)

            def score_b(g, b, s, u, masked):
                t, h = s // HG, s % HG
                pair = s // 2
                if s == 0:
                    pe.wait_ge(m_in, u * 32 + 32)
                if s % 2 == 0:
                    pe.wait_ge(exp_done, u * (SLOTS // 2) + pair + 1)
                out = st[pair % 2][:, s % 2, :]
                if masked:
                    pe.matmul(out, ident16[:, :], nbT[:, b % 2, t, :], start=True, stop=False)
                last = pe.matmul(out, k_stack[g][:, h, t * P:(t + 1) * P], q_stack[g][:, h, :], start=not masked, stop=True)
                if s % 2:
                    last.then_inc(st_full, 1)

            def values(g, t):
                for h in range(HG):
                    last = pe.matmul(av[32 * h:32 * h + 32, :], vw[:, g, t, h, :], pr[:, t % 2, h, :],
                                     start=(t == 0), stop=(t == TB - 1), skip_group_check=True)
                last.then_inc(av_done, 1)

            def all_units(masked):
                for g in range(2):
                    for s in range(SLOTS):
                        score_a(g, 0, s, g, masked)
                    if g == 0:
                        max_rows(nf - 1, 0, 0)
                with pe.Fori(0, B) as b:
                    for g in range(G):
                        u = b * G + g
                        for s in range(SLOTS):
                            score_b(g, b, s, u, masked)
                            score_a((g + 2) % G, b if g < 2 else b + 1, s, u + 2, masked)
                            if s == 2:
                                pe.wait_ge(exp_done, u * (SLOTS // 2) + 2)
                                values((g - 1) % G, TB - 1)
                            elif s > 3 and s % 4 == 3:
                                t = s // 4 - 1
                                pe.wait_ge(exp_done, u * (SLOTS // 2) + 2 * t + 4)
                                if t == 0:
                                    pe.wait_ge(vw_ready, u + 1)
                                    pe.wait_ge(av_free, u + 1)
                                values(g, t)
                            for n, name, piece in pieces_at(g, s):
                                job = b * nj + (nf + n)
                                if name == "m":
                                    max_rows(job, u + 1, (g + 1) % 2)
                                elif name[0] == "o":
                                    output(job, b, int(name[1]), piece)
                                else:
                                    prepare(job, name, b + 1, piece)

            pe.wait_ge(w_in, 16 * 7)
            for n, name in enumerate(FIRST[:-1]):
                if n == 0:
                    pe.wait_ge(set_up, SETUP)
                for piece in range(PIECES[name[0]]):
                    prepare(n, name, 0, piece)
            for t in range(TB - 1):
                values(G - 1, t)
            flagged = pe.value_load(flag[0:1, 0:1], min_val=0, max_val=1)
            with pe.If(flagged > 0):
                all_units(True)
            with pe.Else():
                all_units(False)
            pe.wait_ge(exp_done, B * G * (SLOTS // 2) + 2)
            values(G - 1, TB - 1)
            for c in range(2):
                for piece in range(PIECES["o"]):
                    output(B * nj + nf + c, B, c, piece)

        @block.scalar
        def _(act):
            def evacuate(n, name, b):
                c = int(name[-1]) if name != "m" else 0
                act.wait_ge(misc_full, n + 1)
                if name == "m":
                    act.copy(mfull[:, :], misc[0:HG, :]).then_inc(misc_free, 1)
                elif name[0] == "k":
                    if not (isinstance(b, int) and b == 0):
                        act.wait_ge(k_stored, b * 16)
                    act.activation(kp[:, 0, c, :], misc[:, :], ACT.Identity, bias=bk[:, c:c + 1]).then_inc(k_head, 1)
                else:
                    act.copy(xT[:, c, :], misc[:, :]).then_inc(misc_free, 1)

            def take(u):
                act.wait_ge(av_done, u * TB + TB)
                act.wait_ge(outT_ready, u + 1)
                act.copy(avs[:, :], av[:, :]).then_inc(av_free, 1)

            def send_rows(g, a):
                act.wait_ge(ml_ready, a + 1)
                for r in range(2):
                    act.dma_start(q_stack[g][R4 + r:R4 + r + 1, :, :].bitcast(F32), mrow[:, r, :].bitcast(F32)).then_inc(m_in, 16)

            act.wait_ge(w_in, 16 * 7)
            act.wait_ge(set_up, SETUP)
            for n, name in enumerate(FIRST):
                if name[0] in "kxm":
                    evacuate(n, name, 0)
            send_rows(0, 0)
            with act.Fori(0, B) as b:
                for g in range(G):
                    u = b * G + g
                    for s in range(SLOTS):
                        if s == 6:
                            take(u)
                        if s == 8:
                            send_rows((g + 1) % G, u + 1)
                        if s % 2:
                            pair = s // 2
                            act.wait_ge(st_full, u * (SLOTS // 2) + pair + 1)
                            if pair % 2 == 0:
                                act.wait_ge(av_done, u * TB + pair // 2 + 3)
                            h = 2 * (pair % 2)
                            act.activation(pr[:, pair // 2 % 2, h:h + 2, :], st[pair % 2][:, :, :], ACT.Exp,
                                           scale=DK ** -0.5).then_inc(exp_done, 1)
                        for n, name in jobs_at(g, s):
                            if name[0] in "kxm":
                                evacuate(b * nj + (nf + n), name, b + 1)
            take(B * G)
            act.wait_ge(m_in, 32 * (B * G + 1))

        @block.gpsimd
        def _(pool):
            def split_q(c, n, b):
                pool.wait_ge(misc_free, n + 1)
                if not (isinstance(b, int) and b == 0):
                    pool.wait_ge(q_stored, b * 16)
                pool.tensor_tensor(qp[:, 0, c, :].rearrange("p (t n) -> p t n", n=P), qf[:, c, :].rearrange("p (t n) -> p t n", n=P),
                                   ones[:, :].rearrange("p (a n) -> p a n", a=1).to_broadcast([P, TB, P]), ALU.mult).then_inc(q_head, 1)
                pool.wait_ge(q_head, b * KC + c + 1)
                pool.tensor_tensor(qp[:, 1, c, :], qf[:, c, :], qp[:, 0, c, :].bitcast(F32), ALU.subtract).then_inc(qp_ready, 1)

            def split_rows(n, a):
                pool.wait_ge(misc_free, n + 1)
                if not (isinstance(a, int) and a == 0):
                    pool.wait_ge(m_in, a * 32)
                pool.tensor_tensor(mrow[:, 0, :].rearrange("p (t n) -> p t n", n=P), mfull[:, :].rearrange("p (t n) -> p t n", n=P),
                                   ones[0:HG, :].rearrange("p (a n) -> p a n", a=1).to_broadcast([HG, TB, P]), ALU.mult).then_inc(mh_ready, 1)
                pool.wait_ge(mh_ready, a + 1)
                pool.tensor_tensor(mrow[:, 1, :], mfull[:, :], mrow[:, 0, :].bitcast(F32), ALU.subtract).then_inc(ml_ready, 1)

            def move_values(g, u, n):
                if n is not None:
                    pool.wait_ge(misc_free, n + 1)
                if not isinstance(u, int):
                    pool.wait_ge(av_done, (u - (G - 1)) * TB + 4)
                for t in range(TB):
                    v = vstage[:, t, g * HG * DK:(g + 1) * HG * DK].rearrange("p (h d) -> p h d", d=DK)
                    last = pool.tensor_tensor(vw[:, g, t, :, 0:DK], v, ones[:, 0:HG * DK].rearrange("p (h d) -> p h d", d=DK), ALU.mult)
                last.then_inc(vw_ready, 1)

            def divide(g, u):
                pool.wait_ge(rec_ready, u * TB + TB)
                pool.tensor_tensor(outT[:, g, :], avs[:, :], sums[:, :], ALU.mult).then_inc(outT_ready, 1)

            pool.memset(pr[:, :, :, :], 1.0).then_inc(set_up, 1)
            pool.memset(vw[:, :, :, :, 0:DK], 0.0).then_inc(set_up, 1)
            pool.memset(vw[:, :, :, :, DK:32], 1.0).then_inc(set_up, 1)
            pool.memset(outT[:, :, :], 0.0).then_inc(outT_ready, 1)
            pool.memset(tiny16[:, :], -1.0 / MASKED).then_inc(set_up, 1)
            for c in range(KC):
                split_q(c, FIRST.index(f"q{c}"), 0)
            for g in range(G - 1):
                move_values(g, g, FIRST.index("v1"))
            split_rows(nf - 1, 0)
            with pool.Fori(0, B) as b:
                for g in range(G):
                    u = b * G + g
                    split_rows(b * nj + (nf + [n for n, j in enumerate(JOBS) if j[0] == "m"][g]), u + 1)
                    if g == 0:
                        move_values(G - 1, u + G - 1, None)
                    if g == 1:
                        split_q(1, b * nj + (nf + number("q1")), b + 1)
                        pool.wait_ge(misc_full, b * nj + (nf + number("o1") + 1))
                    divide((g - 1) % G, u)
                    if g == 0:
                        split_q(0, b * nj + (nf + number("q0")), b + 1)
                    for i in {2: (0, 1), 3: (2,)}.get(g, ()):
                        move_values(i, u + (G - g + i), b * nj + (nf + number("v1")))
            divide(G - 1, B * G)

        @block.vector
        def _(dve):
            def normalise(b, mean_b):
                for i in range(TB):
                    t = mean_b * TB + i
                    dve.tensor_scalar(xn[:, i, :], x[:, bass.ds(t, 1), :], mv[:, bass.ds(t, 1), 0],
                                      rstd[:, bass.ds(t, 1)], ALU.subtract, ALU.mult).then_inc(xn_ready, 1)

            def maximum(g, s, a):
                dve.wait_ge(na_full, a * SLOTS + s + 1)
                dve.tensor_reduce(negmax[:, g % 2, s % TB, s // TB:s // TB + 1], na[s % 2][:, :], AX.X, ALU.max,
                                  negate=True).then_inc(max_done, 1)

            def evacuate(n, name, b, a, bx):
                dve.wait_ge(misc_full, n + 1)
                c = int(name[-1]) if name[-1].isdigit() else 0
                if name[0] == "k":
                    dve.wait_ge(k_head, b * KC + c + 1)
                    dve.scalar_tensor_tensor(out=kp[:, 1, c, :], in0=misc[:, :], scalar=bk[:, c:c + 1],
                                             in1=kp[:, 0, c, :].bitcast(F32), op0=ALU.add, op1=ALU.subtract).then_inc(misc_free, 1)
                elif name == "rv":
                    dve.tensor_scalar(rv[:, :], misc[:, :], 0.5 - S, None, ALU.is_gt).then_inc(misc_free, 1)
                elif name[0] == "q":
                    if not (isinstance(b, int) and b == 0):
                        dve.wait_ge(qp_ready, b * KC)
                    dve.scalar_tensor_tensor(out=qf[:, c, :], in0=misc[:, :], scalar=bq[:, c:c + 1], in1=rv[:, :],
                                             op0=ALU.add, op1=ALU.mult).then_inc(misc_free, 1)
                elif name[0] == "v":
                    if not (isinstance(b, int) and b == 0):
                        dve.wait_ge(vw_ready, b * G)
                    dve.tensor_tensor(vstage[:, 2 * c:2 * c + 2, :], misc[:, :].rearrange("p (t n) -> p t n", t=2),
                                      bv[:, :].rearrange("p (a n) -> p a n", a=1).to_broadcast([P, 2, D]), ALU.add).then_inc(misc_free, 1)
                else:
                    t = bx * TB + 2 * c
                    dve.tensor_tensor(x[:, bass.ds(t, 2), :], misc[:, :].rearrange("p (t n) -> p t n", t=2),
                                      x[:, bass.ds(t, 2), :], ALU.add).then_inc(misc_free, 1)

            def invert(u, i):
                if i == 0:
                    dve.wait_ge(av_free, u + 1)
                    dve.memset(tick[:, :], 0.0)
                    dve.stream_shuffle(sums[:, :], avs[:, :], [DK + i % DK for i in range(32)]).then_inc(sums_ready, 1)
                    return
                q = slice((i - 1) * P, i * P)
                dve.wait_ge(sums_ready, u + 1)
                dve.reciprocal(sums[:, q], sums[:, q]).then_inc(rec_ready, 1)

            dve.tensor_copy(ident16[:, :], ident[:, :]).then_inc(set_up, 1)
            for g in range(G):
                dve.memset(k_stack[g][R4:P, :, :].bitcast(F32), 1.0).then_inc(set_up, 1)
                dve.memset(q_stack[g][R4:P, :, :].bitcast(F32), 0.0).then_inc(set_up, 1)
            dve.memset(zrow[:, :], 0.0).then_inc(set_up, 1)
            for i in range(2):
                dve.memset(negmax[:, i, 0, 0:1], 0.0).then_inc(max_done, 1)
                dve.memset(sums[:, i:i + 1], 0.0).then_inc(exp_done, 1)
            dve.wait_ge(max_done, 2)
            dve.wait_ge(exp_done, 2)
            dve.wait_ge(w_in, 16 * 7)
            normalise(0, 0)
            for n, name in enumerate(FIRST[:-1]):
                if name[0] != "x":
                    evacuate(n, name, 0, None, None)
            for g in range(2):
                for s in range(SLOTS):
                    maximum(g, s, g)
            with dve.Fori(0, B) as b:
                for g in range(G):
                    u = b * G + g
                    for s in range(SLOTS):
                        maximum(g + 2, s, u + 2)
                        if s in (7, 9, 11, 13, 15):
                            invert(u, (s - 7) // 2)
                        if (g, s) == (0, 1):
                            normalise(b + 1, (b + 1) % B)
                        for n, name in jobs_at(g, s):
                            if name[0] not in "xm":
                                evacuate(b * nj + (nf + n), name, b + 1, u + 1, (b + (B - 1)) % B)
            for i in range(TB + 1):
                invert(B * G, i)
            for c in range(2):
                evacuate(B * nj + nf + c, f"o{c}", None, None, B - 1)
            dve.wait_ge(misc_free, B * nj + nf + 2)


def self_gates(nc, io, x, mv, rstd, ident, iota8, xT_d, gT_d, weights):
    with ExitStack() as ctx:
        m = Names(nc, ctx, "sg")
        xn = m.sb("xn", [P, 4, D])
        xt = m.sb("xt", [P, KC, B * S])
        ws = m.sb("ws", [P, KC, SH])
        sig, top, topf = m.sb("sig", [P, NT, SH]), m.sb("top", [P, NT, 8]), m.sb("topf", [P, NT, 8])
        topi = m.sb("topi", [P, NT, 8], U32)
        hot = m.sb("hot", [P, STOP, NT, SH])
        kept = m.sb("kept", [P, 2, NT, SH])
        gate = m.sb("gate", [P, NT, SH])
        gT = m.sb("gT", [SH, B * S])
        gh, gl = m.sb("gh", [SH, B * S], F32R), m.sb("gl", [SH, B * S], F32R)
        xtp = [m.ps(f"xtp{i}", [P, KC, P]) for i in range(2)]
        lg = m.ps("lg", [P, NT, SH])
        gtp = [m.ps(f"gtp{i}", [SH, S]) for i in range(2)]
        ws_in_s, xn_ready, xtp_ready, xt_ready, lg_ready, sig_ready, step = (
            m.sem(n) for n in ("ws_in", "xn_ready", "xtp_ready", "xt_ready", "lg_ready", "sig_ready", "step"))
        gate_ready, gtp_ready, gT_ready, stored = (m.sem(n) for n in ("gate_ready", "gtp_ready", "gT_ready", "stored"))
        st6, std, eps = m.sb("st6", [P, NT, 6]), m.sb("std", [P, NT]), m.sb("eps", [P, 1])
        st_ready, stats_ready, std_ready, rstd_ready, eps_set, w_in = (
            m.sem(n) for n in ("st_ready", "stats_ready", "std_ready", "rstd_ready", "eps_set", "w_in"))
        gh_ready, gl_ready = m.sem("gh_ready"), m.sem("gl_ready")
        block = ctx.enter_context(nc.Block())

        @block.gpsimd
        def _(pool):
            for w, name in weights[:-1]:
                pool.dma_start(w[:, :, :], io[name].rearrange("(c p) n -> p c n", p=P)).then_inc(w_in, 16)
            w, name = weights[-1]
            pool.dma_start(w[:, :], io[name]).then_inc(w_in, 16)
            pool.wait_ge(w_in, 16 * len(weights))

        @block.sync
        def _(sp):
            sp.dma_start(ws[:, :, :], io["sWs"].rearrange("(c p) e -> p c e", p=P)).then_inc(ws_in_s, 16)
            for b in range(B):
                sp.wait_ge(xt_ready, (b + 1) * TB)
                sp.dma_start(xT_d.rearrange("(c p) n -> p c n", p=P)[:, :, b * S:(b + 1) * S], xt[:, :, b * S:(b + 1) * S]).then_inc(stored, 16)
            sp.wait_ge(gl_ready, B)
            sp.dma_start(gT_d[0:SH, :], gT[:, :]).then_inc(stored, 16)
            sp.dma_start(gT_d[SH:2 * SH, :], gh[:, :].bitcast(F32)).then_inc(stored, 16)
            sp.dma_start(gT_d[2 * SH:3 * SH, :], gl[:, :].bitcast(F32)).then_inc(stored, 16)
            sp.wait_ge(stored, 16 * (B + 3))

        @block.tensor
        def _(pe):
            def gate_tile(t):
                pe.wait_ge(xt_ready, t + 1)
                for c in range(KC):
                    last = pe.matmul(lg[:, t, :], xt[:, c, t * P:(t + 1) * P], ws[:, c, :], start=(c == 0), stop=(c == KC - 1))
                last.then_inc(lg_ready, 1)

            pe.wait_ge(ws_in_s, 16)
            for t in range(NT):
                pe.wait_ge(xn_ready, t + 1)
                if t >= 2:
                    pe.wait_ge(xt_ready, t - 1)
                for c in range(KC):
                    last = pe.transpose(xtp[t % 2][:, c, :], xn[:, t % 4, c * P:(c + 1) * P], ident[:, :])
                last.then_inc(xtp_ready, 1)
                if t >= 1:
                    gate_tile(t - 1)
            gate_tile(NT - 1)
            pe.wait_ge(gate_ready, 1)
            for b in range(B):
                if b >= 2:
                    pe.wait_ge(gT_ready, b - 1)
                for t in range(TB):
                    last = pe.transpose(gtp[b % 2][:, t * P:(t + 1) * P], gate[:, b * TB + t, :], ident[:, :])
                last.then_inc(gtp_ready, 1)

        @block.scalar
        def _(act):
            def copy_out(t):
                act.wait_ge(xtp_ready, t + 1)
                act.copy(xt[:, :, t * P:(t + 1) * P], xtp[t % 2][:, :, :]).then_inc(xt_ready, 1)

            act.wait_ge(eps_set, 1)
            for t in range(NT):
                if t % TB == 0:
                    b = t // TB
                    act.wait_ge(stats_ready, b + 1)
                    act.activation(std[:, b * TB:(b + 1) * TB], mv[:, b * TB:(b + 1) * TB, 1], ACT.Sqrt, bias=eps[:, 0:1]).then_inc(std_ready, 1)
                if t >= 4:
                    copy_out(t - 4)
            for t in range(NT - 4, NT):
                copy_out(t)
            act.wait_ge(lg_ready, NT)
            act.activation(sig[:, :, :], lg[:, :, :], ACT.Sigmoid).then_inc(sig_ready, 1)
            for b in range(B):
                act.wait_ge(gtp_ready, b + 1)
                act.copy(gT[:, b * S:(b + 1) * S], gtp[b % 2][:, :]).then_inc(gT_ready, 1)

        @block.vector
        def _(dve):
            n = [0]

            def then(ins):
                n[0] += 1
                ins.then_inc(step, 1)
                dve.wait_ge(step, n[0])

            def statistics(b):
                for t in range(b * TB, (b + 1) * TB):
                    dve.bn_stats(st6[:, t, :], x[:, t, :]).then_inc(st_ready, 1)
                for t in range(b * TB, (b + 1) * TB):
                    dve.wait_ge(st_ready, t + 1)
                    last = dve.bn_aggr(mv[:, t, :], st6[:, t, :])
                last.then_inc(stats_ready, 1)

            dve.memset(eps[:, :], EPS).then_inc(eps_set, 1)
            statistics(0)
            for t in range(NT):
                if t % TB == 0:
                    b = t // TB
                    if b + 1 < B:
                        statistics(b + 1)
                    dve.wait_ge(std_ready, b + 1)
                    dve.reciprocal(rstd[:, b * TB:(b + 1) * TB], std[:, b * TB:(b + 1) * TB]).then_inc(rstd_ready, 1)
                    dve.wait_ge(rstd_ready, b + 1)
                if t >= 4:
                    dve.wait_ge(xtp_ready, t - 3)
                dve.tensor_scalar(xn[:, t % 4, :], x[:, t, :], mv[:, t, 0:1], rstd[:, t:t + 1],
                                  ALU.subtract, ALU.mult).then_inc(xn_ready, 1)
            dve.wait_ge(sig_ready, 1)
            for t in range(NT):
                last = dve.max(top[:, t, :], sig[:, t, :])
            then(last)
            for t in range(NT):
                last = dve.max_index(topi[:, t, :], top[:, t, :], sig[:, t, :])
            then(last)
            then(dve.tensor_copy(topf[:, :, :], topi[:, :, :]))
            heads = iota8[:, :].rearrange("p (a e) -> p a e", a=1).to_broadcast([P, NT, SH])
            for j in range(STOP):
                ins = dve.tensor_tensor(hot[:, j, :, :], topf[:, :, j:j + 1].to_broadcast([P, NT, SH]), heads, ALU.is_equal)
            then(ins)
            then(dve.tensor_tensor(kept[:, 0, :, :], hot[:, 0, :, :], hot[:, 1, :, :], ALU.add))
            then(dve.tensor_tensor(kept[:, 1, :, :], kept[:, 0, :, :], hot[:, 2, :, :], ALU.add))
            dve.tensor_tensor(gate[:, :, :], sig[:, :, :], kept[:, 1, :, :], ALU.mult).then_inc(gate_ready, 1)
            for b in range(B):
                n_b = slice(b * S, (b + 1) * S)
                dve.wait_ge(gT_ready, b + 1)
                dve.tensor_copy(gh[:, n_b], gT[:, n_b]).then_inc(gh_ready, 1)
                dve.wait_ge(gh_ready, b + 1)
                dve.tensor_tensor(gl[:, n_b], gT[:, n_b], gh[:, n_b].bitcast(F32), ALU.subtract).then_inc(gl_ready, 1)


def self_attention(nc, io, x, ident, ones, xT_d, gT_d, wq, wk, wv, wo, bo):
    with ExitStack() as ctx:
        m = Names(nc, ctx, "sa")
        C = SH // 2
        H = SDK
        sel = m.sb("sel", [SH, SH * H])
        sel2 = m.sb("sel2", [2 * SH, SH * H], F32R)
        gparts = m.sb("gparts", [2 * SH, S], F32R)
        xT, gT = m.sb("xT", [P, KC, S]), m.sb("gT", [SH, S])
        part = {n: m.sb(n, [P, S], F32R) for n in ("qh", "ql", "kh", "kl")}
        q1, q2, k1, k2 = ([m.sb(f"{n}_{c}", [P, 2, S], F32R) for c in range(C)] for n in ("q1", "q2", "k1", "k2"))
        zrow = m.sb("zrow", [2, S])
        vw = m.sb("vw", [P, C, TB, P])
        negmax = m.sb("negmax", [P, 2, 2, TB])
        parts = m.sb("parts", [P, 2, 2, TB, 2])
        pr = m.sb("pr", [P, TB, 2, S])
        acc = m.sb("acc", [P, 2, S])
        avs, sumS = m.sb("avs", [P, S]), m.sb("sumS", [P, S])
        rec, factor = m.sb("rec", [P, S]), m.sb("factor", [P, S])
        outT = m.sb("outT", [P, C, S])
        tick = m.sb("tick", [P, 1])
        na = [m.ps(f"na{i}", [P, S]) for i in range(2)]
        st = [m.ps(f"st{i}", [P, 2, S]) for i in range(2)]
        av, misc = m.ps("av", [P, S]), m.ps("misc", [P, S])

        set_up, sel_set, sel_in = m.sem("set_up"), m.sem("sel_set"), m.sem("sel_in")
        xT_in, gT_in = m.sem("xT_in"), m.sem("gT_in")
        head_ready = m.sem("head_ready")
        stack_in = [m.sem(f"stack_in{c}") for c in range(C)]
        na_full, max_done, st_full, exp_done = m.sem("na_full"), m.sem("max_done"), m.sem("st_full"), m.sem("exp_done")
        mh_ready, ml_ready = m.sem("mh_ready"), m.sem("ml_ready")
        av_done, av_free, acc_done, outT_ready = m.sem("av_done"), m.sem("av_free"), m.sem("acc_done"), m.sem("outT_ready")
        rec_ready, factor_ready = m.sem("rec_ready"), m.sem("factor_ready")
        misc_full, misc_free = m.sem("misc_full"), m.sem("misc_free")
        out_done = m.sem("out_done")
        block = ctx.enter_context(nc.Block())

        SETUP = 5 + 3 * C
        out = io["out"].rearrange("(t p) d -> p t d", p=P)
        SLOTS = 2 * TB
        LOAD = 16 * 13
        JOBS = []
        for g in range(C):
            if g == 1:
                JOBS += [("q", g, 0, 1), ("k", g, 1, 1), ("sum", g, 2, 1), ("o0", g, 2, 1), ("v", g, 3, 1), ("o1", g, 4, 1)]
            else:
                JOBS += [("q", g, 0, 1), ("k", g, 1, 1), ("sum", g, 2, 1), ("v", g, 3, 1)]
            JOBS += [("m0", g, 4, 1), ("m1", g, 5, 1), ("gate", g, 6, 1)]
        FIRST = ["q", "k", "v"] * 3 + ["m0", "m1"]
        LAST = ["sum", "gate", "o0", "o1"]
        nj, nf = len(JOBS), len(FIRST)

        def job(b, g, name):
            return b * nj + (nf + next(n for n, j in enumerate(JOBS) if j[0] == name and j[1] == g))

        def jobs_at(g, s):
            return [j[0] for j in JOBS if j[1:3] == (g, s)]

        def pieces_at(g, s):
            return [(j[0], s - j[2] + j[3] - 1, j[3]) for j in JOBS if j[1] == g and 0 <= j[2] - s < j[3]]

        def last_job(name):
            return B * nj + nf + LAST.index(name)

        @block.sync
        def _(sp):
            def load_x(n):
                sp.dma_start(xT[:, :, :], xT_d.rearrange("(c p) n -> p c n", p=P)[:, :, bass.ds(n, S)]).then_inc(xT_in, 16)

            def stack(c, pairs):
                for dst, lo, name in pairs:
                    for h in range(2):
                        sp.dma_start(dst[c][lo:lo + H, h, :].bitcast(F32), part[name][h * H:(h + 1) * H, :].bitcast(F32)).then_inc(stack_in[c], 16)

            def load_stacks(c, nq):
                sp.wait_ge(misc_free, nq + 1)
                stack(c, ((q1, 0, "qh"), (q1, H, "ql"), (q2, 0, "qh")))
                sp.dma_start(q2[c][H:H + 2, :, :].bitcast(F32), zrow[:, :].rearrange("p (a n) -> p a n", a=1).to_broadcast([2, 2, S])).then_inc(stack_in[c], 16)
                sp.wait_ge(misc_free, nq + 2)
                stack(c, ((k1, 0, "kh"), (k1, H, "kh"), (k2, 0, "kl")))

            load_x(0)
            sp.wait_ge(sel_set, 3)
            for i in range(2):
                sp.dma_start(sel2[i * SH:(i + 1) * SH, :].bitcast(F32), sel[:, :]).then_inc(sel_in, 16)
            sp.wait_ge(set_up, SETUP)
            for c in range(3):
                load_stacks(c, 3 * c)
            with sp.Fori(0, B) as b:
                for g in range(C):
                    u = b * C + g
                    load_stacks((g + 3) % C, job(b, g, "q"))
                    if g == 0:
                        after = sp.snap(((b + 1) % B) * S)
                        sp.wait_ge(misc_full, job(b, g, "v") + 1)
                        load_x(after)
                    if g == 2:
                        sp.dma_start(out[:, bass.ds(((b + (B - 1)) % B) * TB, TB), :], x[:, bass.ds(((b + (B - 1)) % B) * TB, TB), :]).then_inc(out_done, 16)
                    if g == 1:
                        sp.wait_ge(misc_full, job(b, g, "o1") + 1)
                        sp.dma_start(gT[:, :], gT_d[0:SH, bass.ds(b * S, S)]).then_inc(gT_in, 16)
                        sp.dma_start(gparts[:, :].bitcast(F32), gT_d[SH:3 * SH, bass.ds(b * S, S)]).then_inc(gT_in, 16)
            sp.wait_ge(misc_free, last_job("o1") + 1)
            sp.wait_ge(out_done, 16 * B)
            sp.dma_start(out[:, (B - 1) * TB:, :], x[:, (B - 1) * TB:, :]).then_inc(out_done, 16)
            sp.wait_ge(out_done, 16 * (B + 1))
            for c in range(C):
                sp.wait_ge(stack_in[c], LOAD * (B + 1 if c < 3 else B))
            sp.wait_ge(xT_in, 16 * (B + 1))
            sp.wait_ge(gT_in, 32 * B)

        @block.tensor
        def _(pe):
            def bank_free(n):
                if not (isinstance(n, int) and n == 0):
                    pe.wait_ge(misc_free, n)

            def max_rows(n, a, par, h):
                bank_free(n)
                pe.wait_ge(ml_ready, a * 2 + (h + 1))
                for t in range(TB):
                    last = pe.matmul(misc[H:H + 2, t * P:(t + 1) * P], parts[:, par, h, t, :], ident[:, :], start=True, stop=True)
                last.then_inc(misc_full, 1)

            def project(n, name, c, b, piece=0, count=1):
                if piece == 0:
                    bank_free(n)
                    if name == "q":
                        pe.wait_ge(xT_in, b * 16 + 16)
                if name == "v":
                    for t in range(piece * TB // count, (piece + 1) * TB // count):
                        for i in range(KC):
                            last = pe.matmul(misc[:, t * P:(t + 1) * P], xT[:, i, t * P:(t + 1) * P], wv[:, i, c * P:(c + 1) * P],
                                             start=(i == 0), stop=(i == KC - 1))
                else:
                    w = wq if name == "q" else wk
                    for i in range(piece * KC // count, (piece + 1) * KC // count):
                        last = pe.matmul(misc[:, :], w[:, i, c * P:(c + 1) * P], xT[:, i, :], start=(i == 0), stop=(i == KC - 1))
                if piece == count - 1:
                    last.then_inc(misc_full, 1)

            def sums(n, u):
                bank_free(n)
                pe.wait_ge(acc_done, u * 3 + 3)
                for h in range(2):
                    last = pe.matmul(misc[h * H:(h + 1) * H, :], ones[:, 0:H], acc[:, h, :], start=True, stop=True, skip_group_check=True)
                last.then_inc(misc_full, 1)

            def gates(n, c):
                bank_free(n)
                pe.matmul(misc[:, :], sel2[:, c * P:(c + 1) * P], gparts[:, :], start=True, stop=True).then_inc(misc_full, 1)

            def output(n, b, i, pieces):
                if 0 in pieces:
                    bank_free(n)
                    pe.wait_ge(outT_ready, b * C + 2)
                for t in pieces:
                    tok = (2 * i + t) * P
                    out = misc[:, t * D:(t + 1) * D]
                    for c in range(C):
                        pe.matmul(out, outT[:, c, tok:tok + P], wo[:, c, :], start=(c == 0), stop=False)
                    last = pe.matmul(out, gT[:, tok:tok + P], bo[:, :], start=False, stop=True)
                if 1 in pieces:
                    last.then_inc(misc_full, 1)

            def score_a(c, b, s, a):
                h, t = s // TB, s % TB
                if s == 0:
                    pe.wait_ge(stack_in[c], b * LOAD + LOAD)
                pe.wait_ge(max_done, a * SLOTS + (s + 1))
                pe.matmul(na[s % 2][:, :], q1[c][:, h, t * P:(t + 1) * P], k1[c][:, h, :], start=True, stop=False)
                pe.matmul(na[s % 2][:, :], q2[c][:, h, t * P:(t + 1) * P], k2[c][:, h, :], start=False, stop=True).then_inc(na_full, 1)

            def score_b(c, s, u):
                t, h = s // 2, s % 2
                if h == 0:
                    pe.wait_ge(exp_done, u * TB + (t + 1))
                out = st[t % 2][:, h, :]
                pe.matmul(out, k1[c][:, h, t * P:(t + 1) * P], q1[c][:, h, :], start=True, stop=False)
                last = pe.matmul(out, k2[c][:, h, t * P:(t + 1) * P], q2[c][:, h, :], start=False, stop=True)
                if h:
                    last.then_inc(st_full, 1)

            def values(c, t):
                for h in range(2):
                    last = pe.matmul(av[h * H:(h + 1) * H, :], vw[:, c, t, h * H:(h + 1) * H], pr[:, t, h, :],
                                     start=(t == 0), stop=(t == TB - 1), skip_group_check=True)
                last.then_inc(av_done, 1)

            pe.wait_ge(set_up, SETUP)
            pe.wait_ge(sel_in, 32)
            for n, name in enumerate(FIRST[:-2]):
                project(n, name, n // 3, 0)
            for t in range(TB - 1):
                values(C - 1, t)
            for a in range(2):
                for s in range(SLOTS):
                    score_a(a, 0, s, a)
                if a == 0:
                    for h in range(2):
                        max_rows(nf - 2 + h, 0, 0, h)
            with pe.Fori(0, B) as b:
                for g in range(C):
                    u = b * C + g
                    for s in range(SLOTS):
                        if s == 0:
                            pe.wait_ge(misc_free, b * nj + (nf if g == 0 else nf + next(n for n, j in enumerate(JOBS) if j[:2] == ("m1", g - 1)) + 1))
                        score_b(g, s, u)
                        score_a((g + 2) % C, b if g < 2 else b + 1, s, u + 2)
                        if s == 1:
                            pe.wait_ge(exp_done, u * TB + 2)
                            values((g - 1) % C, TB - 1)
                        if s >= 3 and s % 2:
                            t = s // 2 - 1
                            pe.wait_ge(exp_done, u * TB + (t + 3))
                            if t == 0:
                                pe.wait_ge(av_free, u + 1)
                            values(g, t)
                        for name, piece, count in pieces_at(g, s):
                            n = job(b, g, name)
                            if name[0] == "m":
                                max_rows(n, u + 1, (g + 1) % 2, int(name[1]))
                            elif name == "sum":
                                sums(n, u)
                            elif name == "gate":
                                if g == 1:
                                    pe.wait_ge(gT_in, b * 32 + 32)
                                gates(n, (g - 1) % C)
                            elif name[0] == "o":
                                output(n, b, int(name[1]), (0, 1) if count == 1 else (piece,))
                            else:
                                project(n, name, (g + 3) % C, b if g == 0 else b + 1, piece, count)
            pe.wait_ge(exp_done, B * C * TB + 2)
            values(C - 1, TB - 1)
            sums(last_job("sum"), B * C)
            gates(last_job("gate"), C - 1)
            for i in range(2):
                output(last_job(f"o{i}"), B, i, (0, 1))

        @block.scalar
        def _(act):
            def head(n, name, k, prev):
                act.wait_ge(misc_full, n + 1)
                if prev is not None:
                    act.wait_ge(*prev)
                act.copy(part[name + "h"][:, :], misc[:, :]).then_inc(head_ready, 1)

            def v_out(n, c):
                act.wait_ge(misc_full, n + 1)
                act.copy(vw[:, c, :, :], misc[:, :].rearrange("p (t n) -> p t n", n=P)).then_inc(misc_free, 1)

            def sum_out(n, u):
                act.wait_ge(misc_full, n + 1)
                act.wait_ge(rec_ready, u * 2 + 2)
                act.copy(sumS[:, :], misc[:, :]).then_inc(misc_free, 1)

            def take(u):
                act.wait_ge(av_done, u * TB + 4)
                act.wait_ge(outT_ready, u + 1)
                act.copy(avs[:, :], av[:, :]).then_inc(av_free, 1)

            def m_out(n, c, h):
                act.wait_ge(misc_full, n + 1)
                act.copy(q2[c][H:H + 2, h, :], misc[H:H + 2, :]).then_inc(misc_free, 1)

            act.wait_ge(set_up, SETUP)
            for n, name in enumerate(FIRST[:-2]):
                c = n // 3
                if name == "v":
                    v_out(n, c)
                else:
                    head(n, name, None, (stack_in[c - 1], LOAD) if c else None)
            for h in range(2):
                m_out(nf - 2 + h, 0, h)
            with act.Fori(0, B) as b:
                for g in range(C):
                    u = b * C + g
                    for s in range(SLOTS):
                        if s % 2:
                            t = s // 2
                            act.wait_ge(st_full, u * TB + (t + 1))
                            act.wait_ge(av_done, u * TB + (t + 1))
                            act.wait_ge(acc_done, u * 3 + max(t, 1))
                            act.activation(pr[:, t, :, :], st[t % 2][:, :, :], ACT.Exp, scale=H ** -0.5).then_inc(exp_done, 1)
                        if s == 2:
                            take(u)
                        for name in jobs_at(g, s):
                            n = job(b, g, name)
                            if name == "sum":
                                sum_out(n, u)
                            elif name in "qk":
                                head(n, name, None, (stack_in[(g + 2) % C], b * LOAD + (2 * LOAD if g >= 2 else LOAD)))
                            elif name == "v":
                                v_out(n, (g + 3) % C)
                            elif name[0] == "m":
                                m_out(n, (g + 1) % C, int(name[1]))
            take(B * C)
            sum_out(last_job("sum"), B * C)

        @block.gpsimd
        def _(pool):
            pool.memset(pr[:, :, :, :], 1.0).then_inc(set_up, 1)
            pool.memset(vw[:, :, :, :], 0.0).then_inc(set_up, 1)
            pool.memset(outT[:, :, :], 0.0).then_inc(outT_ready, 1)
            pool.memset(gT[:, :], 0.0).then_inc(set_up, 1)
            for i in range(3):
                pool.memset(acc[:, :, i * P:(i + 1) * P] if i < 2 else acc[:, :, 2 * P:S], 1.0).then_inc(acc_done, 1)
            pool.memset(sel[:, :], 1.0).then_inc(sel_set, 1)
            pool.wait_ge(sel_set, 1)
            pool.affine_select(out=sel[:, :], in_=sel[:, :], compare_op=ALU.is_ge, fill=0.0,
                               base=0, pattern=[[1, SH * H]], channel_multiplier=-H).then_inc(sel_set, 1)
            pool.wait_ge(sel_set, 2)
            pool.affine_select(out=sel[:, :], in_=sel[:, :], compare_op=ALU.is_ge, fill=0.0,
                               base=H - 1, pattern=[[-1, SH * H]], channel_multiplier=H).then_inc(sel_set, 1)
            def gated(c, u):
                pool.wait_ge(factor_ready, u + 1)
                pool.wait_ge(av_free, u + 1)
                pool.tensor_tensor(outT[:, c, :], avs[:, :], factor[:, :], ALU.mult).then_inc(outT_ready, 1)

            with pool.Fori(0, B) as b:
                for g in range(C):
                    u = b * C + g
                    pool.wait_ge(misc_full, job(b, g, "sum") + 1)
                    pool.wait_ge(exp_done, u * TB + 4)
                    pool.tensor_tensor(acc[:, :, :], pr[:, 0, :, :], pr[:, 1, :, :], ALU.add).then_inc(acc_done, 1)
                    for t in (2, 3):
                        pool.wait_ge(exp_done, u * TB + (t + 3))
                        pool.wait_ge(acc_done, u * 3 + (t + 2))
                        pool.tensor_tensor(acc[:, :, :], acc[:, :, :], pr[:, t, :, :], ALU.add).then_inc(acc_done, 1)
                        if t == 2:
                            gated((g - 1) % C, u)
            gated(C - 1, B * C)

        @block.vector
        def _(dve):
            def maximum(par, s, a):
                dve.wait_ge(na_full, a * SLOTS + (s + 1))
                h, t = s // TB, s % TB
                dve.tensor_reduce(negmax[:, par, h, t:t + 1], na[s % 2][:, :], AX.X, ALU.max, negate=True).then_inc(max_done, 1)
                if t == TB - 1:
                    dve.wait_ge(max_done, a * SLOTS + (s + 3))
                    dve.tensor_copy(parts[:, par, h, :, 0].bitcast(F32R), negmax[:, par, h, :]).then_inc(mh_ready, 1)
                    dve.wait_ge(mh_ready, a * 2 + (h + 1))
                    dve.tensor_tensor(parts[:, par, h, :, 1].bitcast(F32R), negmax[:, par, h, :], parts[:, par, h, :, 0], ALU.subtract).then_inc(ml_ready, 1)

            def rest(n, name, k):
                dve.wait_ge(head_ready, k + 1)
                dve.tensor_tensor(part[name + "l"][:, :], misc[:, :], part[name + "h"][:, :].bitcast(F32), ALU.subtract).then_inc(misc_free, 1)

            def reciprocal(n, u, i):
                dve.wait_ge(misc_free, n + 1)
                half = slice(i * S // 2, (i + 1) * S // 2)
                dve.reciprocal(rec[:, half], sumS[:, half]).then_inc(rec_ready, 1)

            def gate(n, u):
                dve.wait_ge(misc_full, n + 1)
                dve.wait_ge(rec_ready, u * 2 + 4)
                dve.wait_ge(outT_ready, u + 1)
                dve.tensor_tensor(factor[:, :], misc[:, :], rec[:, :], ALU.mult).then_inc(factor_ready, 1)
                dve.wait_ge(factor_ready, u + 1)
                dve.memset(tick[:, :], 0.0).then_inc(misc_free, 1)

            def add(n, i, b):
                dve.wait_ge(misc_full, n + 1)
                t = b * TB + 2 * i
                tiles = x[:, t:t + 2, :] if isinstance(b, int) else x[:, bass.ds(t, 2), :]
                dve.tensor_tensor(tiles, misc[:, :].rearrange("p (t n) -> p t n", t=2), tiles, ALU.add).then_inc(misc_free, 1)

            for c in range(C):
                dve.memset(k2[c][H:P, :, :].bitcast(F32), 1.0).then_inc(set_up, 1)
                dve.memset(q2[c][H:P, :, :].bitcast(F32), 0.0).then_inc(set_up, 1)
                dve.memset(q1[c][H:P, 0, 0:1].bitcast(F32), 0.0).then_inc(set_up, 1)
            dve.memset(zrow[:, :], 0.0).then_inc(set_up, 1)
            dve.memset(gparts[:, :].bitcast(F32), 0.0).then_inc(set_up, 1)
            for i in range(2):
                dve.memset(negmax[:, i, 0, 0:1], 0.0).then_inc(max_done, 1)
                dve.memset(factor[:, i:i + 1], 0.0).then_inc(exp_done, 1)
                dve.memset(rec[:, i:i + 1], 0.0).then_inc(rec_ready, 1)
            dve.wait_ge(max_done, 2)
            dve.wait_ge(exp_done, 2)
            dve.wait_ge(rec_ready, 2)
            k = 0
            for n, name in enumerate(FIRST[:-2]):
                if name != "v":
                    rest(n, name, k)
                    k += 1
            for a in range(2):
                for s in range(SLOTS):
                    maximum(a, s, a)
            with dve.Fori(0, B) as b:
                for g in range(C):
                    u = b * C + g
                    for s in range(SLOTS):
                        maximum(g % 2, s, u + 2)
                        if s in (3, 4):
                            reciprocal(job(b, g, "sum"), u, s - 3)
                        for name in jobs_at(g, s):
                            n = job(b, g, name)
                            if name in "qk":
                                rest(n, name, u * 2 + (6 + "qk".index(name)))
                            elif name == "gate":
                                gate(n, u)
                            elif name[0] == "o":
                                add(n, int(name[1]), (b + (B - 1)) % B)
            for i in range(2):
                reciprocal(last_job("sum"), B * C, i)
            gate(last_job("gate"), B * C)
            for i in range(2):
                add(last_job(f"o{i}"), i, B - 1)
            dve.wait_ge(misc_free, last_job("o1") + 1)


def build(nc, io):
    with ExitStack() as ctx:
        m = Names(nc, ctx, "all")
        ident, before, ones = m.sb("ident", [P, P]), m.sb("before", [P, P]), m.sb("ones", [P, P])
        iota8 = m.sb("iota8", [P, E])
        x = m.sb("x", [P, NT, D])
        stats = m.sb("stats", [P, NT, 6])
        mv, rstd = m.sb("mv", [P, NT, 2]), m.sb("rstd", [P, NT])
        weight = m.sb("weight", [P, TOPK, NT])
        place = m.sb("place", [P, TOPK, NT], U32)
        tile_at = m.sb("tile_at", [P, E + 1], I32)
        flag = m.sb("flag", [P, 1], I32)
        rows = nc.dram_tensor("expert_rows", ((MAXT + 1) * P, D), F32).ap()
        outs = nc.dram_tensor("expert_outs", (MAXT * P, D), F32).ap()
        bias = nc.dram_tensor("mask_bias", (2 * B * S, S), BF16).ap()
        q_parts = nc.dram_tensor("q_parts", (2, D, S), F32).ap()
        k_parts = nc.dram_tensor("k_parts", (2, D, S), F32).ap()
        xT_d = nc.dram_tensor("normed_T", (D, B * S), F32).ap()
        gT_d = nc.dram_tensor("gates_T", (3 * SH, B * S), F32).ap()

        constants(nc, ident, before, ones, iota8)
        feature_attention(nc, io["x"], io["ctxT"], x, stats, ident)
        with ExitStack() as c2:
            w = Names(nc, c2, "moe")
            gu_w = [w.sb(f"gu_w{i}", [P, KC, 2 * F]) for i in range(2)]
            dn_w = [w.sb(f"dn_w{i}", [P, FC, D]) for i in range(2)]
            w_in = [w.sem(f"w_in{i}") for i in range(2)]
            with ExitStack() as c3:
                xn = Names(nc, c3, "all").sb("xn", [P, NT, D])
                route(nc, io, rows, outs, x, stats, ident, before, ones, iota8, xn, weight, place, tile_at, gu_w, dn_w, w_in)
            experts(nc, io, rows, outs, ident, ones, tile_at, bias, flag, gu_w, dn_w, w_in)
        with ExitStack() as c2:
            w = Names(nc, c2, "cross")
            weights = {n: w.sb(n, [P, KC, D]) for n in ("wq", "wk", "wv")}
            weights["wo"] = w.sb("wo", [P, G, D])
            weights["bq"], weights["bk"], weights["bv"] = w.sb("bq", [P, KC]), w.sb("bk", [P, KC]), w.sb("bv", [P, D])
            ctxT = w.sb("ctxT", [P, KC, S])
            w_in, ctx_in = w.sem("w_in"), w.sem("ctx_in")
            combine(nc, io, outs, x, weight, place, mv, rstd, weights, ctxT, w_in, ctx_in)
            cross_attention(nc, io, x, mv, rstd, ident, ones, bias, flag, q_parts, k_parts, weights, ctxT, w_in, ctx_in)
        with ExitStack() as c2:
            w = Names(nc, c2, "self")
            wq, wk, wv = (w.sb(n, [P, KC, SH * SDK]) for n in ("wq", "wk", "wv"))
            wo, bo = w.sb("wo", [P, SH * SDK // P, D]), w.sb("bo", [SH, D])
            self_gates(nc, io, x, mv, rstd, ident, iota8, xT_d, gT_d,
                       ((wq, "sWq"), (wk, "sWk"), (wv, "sWv"), (wo, "sWo"), (bo, "sbo")))
            self_attention(nc, io, x, ident, ones, xT_d, gT_d, wq, wk, wv, wo, bo)


def cross_output_rows(wo, bo):
    import numpy as np
    rows = np.zeros((HEADS, 32, D), np.float32)
    rows[:, :DK, :] = np.asarray(wo).T.reshape(HEADS, DK, D)
    rows[0, DK, :] = np.asarray(bo)
    return rows.reshape(HEADS * 32, D)


def layout(a):
    import numpy as np
    f = lambda v: np.ascontiguousarray(v)
    return {
        "x": f(np.reshape(a["x"], (B * S, D))),
        "ctxT": f(np.reshape(a["ctx_1024"], (B * S, D)).T),
        "gateT": f(np.asarray(a["L0_ffn_gate_w"]).T),
        "gateupT": f(np.transpose(a["L0_ffn_gate_up_proj"], (0, 2, 1))),
        "downT": f(np.transpose(a["L0_ffn_down_proj"], (0, 2, 1))),
        "masks": f(np.concatenate([np.reshape(a["mask_BxSxS2_if1"], (B * S, S)),
                                   np.reshape(np.transpose(a["mask_BxSxS2_if1"], (0, 2, 1)), (B * S, S))])),
        "wqT": f(np.asarray(a["L1_xattn_Wq"]).T), "bq": f(a["L1_xattn_bq"]),
        "wkT": f(np.asarray(a["L1_xattn_Wk"]).T), "bk": f(a["L1_xattn_bk"]),
        "wvT": f(np.asarray(a["L1_xattn_Wv"]).T), "bv": f(a["L1_xattn_bv"]),
        "sWq": f(a["L1_ffn_Wq"]), "sWk": f(np.asarray(a["L1_ffn_Wkv"])[:, :SH * SDK]),
        "sWv": f(np.asarray(a["L1_ffn_Wkv"])[:, SH * SDK:]), "sWs": f(a["L1_ffn_Ws"]),
        "sWo": f(np.reshape(a["L1_ffn_Wo"], (SH * SDK, D))), "sbo": f(a["L1_ffn_bo"]),
        "woT": cross_output_rows(a["L1_xattn_Wo"], a["L1_xattn_bo"]),
    }


def kernel(**inputs):
    import numpy as np
    import concourse.bacc as bacc
    from concourse.bass_utils import run_bass_kernel_spmd

    nc = bacc.Bacc("TRN2", target_bir_lowering=False, num_devices=1)
    arrays = layout({name: np.asarray(v) for name, v in inputs.items()})
    io = {name: nc.dram_tensor(name, v.shape, mybir.dt.from_np(v.dtype), kind="ExternalInput").ap() for name, v in arrays.items()}
    io["out"] = nc.dram_tensor("out", (B * S, D), F32, kind="ExternalOutput").ap()
    build(nc, io)
    result = run_bass_kernel_spmd(nc, [arrays], core_ids=[0])
    return result.results[0]["out"].reshape(B, S, D)
```
